# Optimizing a Trainium2 kernel written in Bass

```python
import numpy as np
import jax
import jax.numpy as jnp

def _softmax(x, axis=-1):
    return jax.nn.softmax(x, axis=axis)

def _gelu(x):
    return jax.nn.gelu(x, approximate=True)

def _silu(x):
    return jax.nn.silu(x)

def _sigmoid(x):
    return jax.nn.sigmoid(x)

def _layernorm(x, axis=-1, eps=1e-05):
    m = jnp.mean(x, axis=axis, keepdims=True)
    v = jnp.var(x, axis=axis, keepdims=True)
    return (x - m) / jnp.sqrt(v + eps)

def _scatter_add(tgt, idx, src, axis=0):
    return tgt.at[idx].add(src)

def _segment_sum(src, seg, n):
    return jax.ops.segment_sum(src, seg, n)
kernel_name = 'mk_adj_ffn_d1_adj_r2_1599d5'

def setup_inputs(seed: int=0):
    np.random.seed(seed)
    _w = jnp.asarray

    def _rec_inputs():
        import jax
        import jax.numpy as jnp
        _gk = jax.random.key(seed)
        x = -0.0002928 + 1 * jax.random.normal(jax.random.fold_in(_gk, 1), (8, 1024, 128), jnp.float32)
        _a = jax.random.bernoulli(jax.random.fold_in(_gk, 2), 0.00195312, (8, 1024, 1024))
        _a = jnp.logical_or(_a, jnp.swapaxes(_a, -1, -2))
        _a = jnp.logical_or(_a, jnp.eye(1024, dtype=bool))
        _af = _a.astype(jnp.float32)
        _af = _af * jax.random.uniform(jax.random.fold_in(_gk, 3), (8, 1024, 1024), jnp.float32, 0.05, 1)
        adj = _af
        return (x, adj)
    x, adj = _rec_inputs()

    def _L0_gnn_setup():
        import jax, jax.numpy as jnp
        import numpy as np
        B, N, D, H = (8, 1024, 128, 512)
        RMS_EPS = 1e-06

        def _rmsnorm(h, w, eps=RMS_EPS):
            var = jnp.mean(jnp.square(h), axis=-1, keepdims=True)
            return h * jax.lax.rsqrt(var + eps) * w
        key = jax.random.key(seed)
        ks = jax.random.split(key, 5)
        x = jax.random.normal(ks[0], (B, N, D), dtype=jnp.float32)
        adjacency = jax.random.uniform(ks[1], (B, N, N), dtype=jnp.float32)
        epsilon = jnp.zeros((), dtype=jnp.float32)
        W1 = jax.random.normal(ks[2], (D, H), dtype=jnp.float32) * (1.0 / np.sqrt(D))
        b1 = jnp.zeros((H,), dtype=jnp.float32)
        rms_weight = jnp.ones((H,), dtype=jnp.float32)
        W2 = jax.random.normal(ks[3], (H, D), dtype=jnp.float32) * (1.0 / np.sqrt(H))
        b2 = jnp.zeros((D,), dtype=jnp.float32)
        return {'x': x, 'adjacency': adjacency, 'epsilon': epsilon, 'W1': W1, 'b1': b1, 'rms_weight': rms_weight, 'W2': W2, 'b2': b2}
    _L0_gnn_all = _L0_gnn_setup()
    _L0_gnn_in = {k: v for k, v in _L0_gnn_all.items() if k in ('epsilon', 'W1', 'b1', 'rms_weight', 'W2', 'b2')}
    del _L0_gnn_all

    def _L0_ffn_setup():
        import jax, jax.numpy as jnp
        import numpy as np
        B, S, D, H, E, K = (8, 4096, 128, 512, 8, 2)
        key = jax.random.key(seed)
        ks = jax.random.split(key, 7)
        s_in = 1.0 / np.sqrt(D)
        s_hid = 1.0 / np.sqrt(H)
        return {'x': jax.random.normal(ks[0], (B, S, D), dtype=jnp.float32), 'Wg': jax.random.uniform(ks[1], (E, D), jnp.float32, -s_in, s_in), 'bg': jax.random.uniform(ks[2], (E,), jnp.float32, -s_in, s_in), 'W1': jax.random.uniform(ks[3], (E, H, D), jnp.float32, -s_in, s_in), 'b1': jax.random.uniform(ks[4], (E, H), jnp.float32, -s_in, s_in), 'W2': jax.random.uniform(ks[5], (E, D, H), jnp.float32, -s_hid, s_hid), 'b2': jax.random.uniform(ks[6], (E, D), jnp.float32, -s_hid, s_hid)}
    _L0_ffn_all = _L0_ffn_setup()
    _L0_ffn_in = {k: v for k, v in _L0_ffn_all.items() if k in ('Wg', 'bg', 'W1', 'b1', 'W2', 'b2')}
    del _L0_ffn_all
    return {'x': x, 'adj': adj, 'L0_gnn_epsilon': _L0_gnn_in['epsilon'], 'L0_gnn_W1': _L0_gnn_in['W1'], 'L0_gnn_b1': _L0_gnn_in['b1'], 'L0_gnn_rms_weight': _L0_gnn_in['rms_weight'], 'L0_gnn_W2': _L0_gnn_in['W2'], 'L0_gnn_b2': _L0_gnn_in['b2'], 'L0_ffn_Wg': _L0_ffn_in['Wg'], 'L0_ffn_bg': _L0_ffn_in['bg'], 'L0_ffn_W1': _L0_ffn_in['W1'], 'L0_ffn_b1': _L0_ffn_in['b1'], 'L0_ffn_W2': _L0_ffn_in['W2'], 'L0_ffn_b2': _L0_ffn_in['b2']}

def reference(x, adj, L0_gnn_epsilon, L0_gnn_W1, L0_gnn_b1, L0_gnn_rms_weight, L0_gnn_W2, L0_gnn_b2, L0_ffn_Wg, L0_ffn_bg, L0_ffn_W1, L0_ffn_b1, L0_ffn_W2, L0_ffn_b2):
    import jax
    import jax.numpy as jnp

    def _L0_gnn_ref(x, adjacency, epsilon, W1, b1, rms_weight, W2, b2):
        import jax, jax.numpy as jnp
        import numpy as np
        B, N, D, H = (8, 1024, 128, 512)
        RMS_EPS = 1e-06

        def _rmsnorm(h, w, eps=RMS_EPS):
            var = jnp.mean(jnp.square(h), axis=-1, keepdims=True)
            return h * jax.lax.rsqrt(var + eps) * w
        neighbor_sum = jnp.einsum('bnm,bmd->bnd', adjacency, x)
        agg = epsilon * x + neighbor_sum
        h = jnp.einsum('bnd,dh->bnh', agg, W1) + b1
        h = jax.nn.silu(_rmsnorm(h, rms_weight))
        out = jnp.einsum('bnh,hd->bnd', h, W2) + b2
        return out

    def _L0_ffn_ref(x, Wg, bg, W1, b1, W2, b2):
        import jax, jax.numpy as jnp
        import numpy as np
        B, S, D, H, E, K = (8, 4096, 128, 512, 8, 2)
        gate_scores = jnp.einsum('bsd,ed->bse', x, Wg) + bg
        topk_scores, topk_idx = jax.lax.top_k(gate_scores, K)
        topk_probs = jax.nn.softmax(topk_scores, axis=-1)
        combine = jnp.sum(topk_probs[..., None] * jax.nn.one_hot(topk_idx, E, dtype=x.dtype), axis=-2)
        out = jnp.zeros_like(x)
        for e in range(E):
            h = jax.nn.relu(jnp.einsum('bsd,hd->bsh', x, W1[e]) + b1[e])
            y = jnp.einsum('bsh,dh->bsd', h, W2[e]) + b2[e]
            out = out + combine[..., e:e + 1] * y
        return out
    x = x + _L0_gnn_ref(_layernorm(x, axis=-1), adj, L0_gnn_epsilon, L0_gnn_W1, L0_gnn_b1, L0_gnn_rms_weight, L0_gnn_W2, L0_gnn_b2)
    x = x + _L0_ffn_ref(_layernorm(x, axis=-1), L0_ffn_Wg, L0_ffn_bg, L0_ffn_W1, L0_ffn_b1, L0_ffn_W2, L0_ffn_b2)
    return x

_drawn_inputs = setup_inputs


def setup_inputs(seed=0):
    import zlib

    import numpy as np

    out = dict(_drawn_inputs(seed))
    spreads = {'L0_gnn_b1': (0.0, 0.1), 'L0_gnn_rms_weight': (1.0, 0.2), 'L0_gnn_b2': (0.0, 0.1)}
    factors = {'L0_ffn_b1': 4.563, 'L0_ffn_b2': 3.608}
    for name, (base, spread) in spreads.items():
        noise = np.random.default_rng([zlib.crc32(name.encode()), seed]).standard_normal(out[name].shape)
        drawn = base * np.exp(spread * noise) if base else spread * noise
        out[name] = jnp.asarray(drawn.astype(out[name].dtype))
    for name, factor in factors.items():
        out[name] = (out[name] * factor).astype(out[name].dtype)
    return out
```

```python
from contextlib import ExitStack

import numpy as np
import concourse.bass as bass
from concourse import mybir

FP32 = mybir.dt.float32
BF16 = mybir.dt.bfloat16
I32 = mybir.dt.int32
ALU = mybir.AluOpType
ACT = mybir.ActivationFunctionType
AX = mybir.AxisListType
P = 128


def build(nc, x, adj, eps, W1, b1, rms_w, W2, b2, Wg, bg, F1, fb1, F2, fb2, out):
    B, N, D = x.shape
    H = W1.shape[1]
    E = Wg.shape[0]
    TOK = B * N
    NT = TOK // P
    TPB = N // P
    GT = 4
    GTOK = GT * P
    NG = NT // GT
    GPB = TPB // GT
    assert GPB == 2
    HC = H // P
    TILE = 256
    J = TILE // P
    NTILE = (2 * TOK + E * (TILE - 1)) // TILE
    MAXT = TOK // TILE
    R = TOK + TILE
    SPARE = NTILE - 2 * TOK // TILE
    ROW = D + 1
    NOWHERE = 1.0e6
    CW1, CB1, CW2, CB2 = 0, H, H + HC, H + HC + H
    WROW = CB2 + D
    BIG = 3.0e38

    slots = nc.dram_tensor("slots", [E * R + SPARE * TILE, ROW], FP32, kind="Internal").ap()
    pairs_out = nc.dram_tensor("pairs_out", [2 * TOK, D], FP32, kind="Internal").ap()

    ctx = ExitStack()
    with ctx:
        def sb(name, shape, dt=FP32):
            return ctx.enter_context(nc.sbuf_tensor(name, shape, dt))

        def sem(name):
            return ctx.enter_context(nc.semaphore(name))

        x_all = sb("x_all", [P, NT, D])
        adj_in = [sb(f"adj_in{i}", [P, GT, N]) for i in range(2)]
        adjT = sb("adjT", [P, 4, GTOK])
        xn = sb("xn", [P, TPB, D])
        aggT = [sb(f"aggT{i}", [P, GTOK]) for i in range(2)]
        hb = sb("hb", [P, GT, H])
        hn = sb("hn", [P, GT, H])
        siluT = sb("siluT", [P, HC, GTOK])
        rows = [sb(f"rows{i}", [P, 2, GT, ROW]) for i in range(2)]
        xn2T = sb("xn2T", [P, GTOK])
        weights = sb("weights", [P, E, WROW])
        W1s = sb("W1s", [P, H])
        W2s = sb("W2s", [P, HC, D])
        b1s = sb("b1s", [P, H])
        b2s = sb("b2s", [P, D])
        bgs = sb("bgs", [P, E])
        epss = sb("epss", [P, 1])
        NS = HC + E * HC + E
        small = sb("small", [NS, D])
        smallT = sb("smallT", [P, NS])
        rmsT, fb1T, WgT = smallT[:, 0:HC], smallT[:, HC:HC + E * HC], smallT[:, HC + E * HC:NS]
        ident = sb("ident", [P, P])
        eps_ident = sb("eps_ident", [P, P])
        earlier = sb("earlier", [P, P], BF16)
        ones = sb("ones", [P, P], BF16)
        minus_half = sb("minus_half", [P, TPB])
        ln_eps = sb("ln_eps", [P, TPB])
        rms_eps = sb("rms_eps", [P, TPB])
        falling = sb("falling", [P, GT, E])
        place_id = sb("place_id", [P, 2, NT])
        pad_rows = sb("pad_rows", [P, J, ROW])
        ss = sb("ss", [P, GT])
        rms_var = sb("rms_var", [P, GT])
        rms_rstd = sb("rms_rstd", [P, GT])
        st1 = sb("st1", [P, TPB, 6])
        mv1 = sb("mv1", [P, TPB, 2])
        ve1 = sb("ve1", [P, TPB])
        rstd1 = sb("rstd1", [P, TPB])
        st2 = sb("st2", [P, GT, 6])
        mv2 = sb("mv2", [P, GT, 2])
        ve2 = sb("ve2", [P, GT])
        rstd2 = sb("rstd2", [P, GT])
        score = sb("score", [P, GT, E])
        top = sb("top", [P, 2, GT])
        first_of = sb("first_of", [P, 2, GT])
        tied = sb("tied", [P, GT, E])
        rest = sb("rest", [P, GT, E])
        onehot = sb("onehot", [P, 2, GT, E])
        both = sb("both", [P, GT + 1, E], BF16)
        base = sb("base", [P, E])
        base0 = sb("base0", [P, E])
        place = sb("place", [P, GT, E])
        picked = sb("picked", [P, 2, GT, E])
        dest = [sb(f"dest{i}", [P, 2, GT], I32) for i in range(2)]
        gap = sb("gap", [P, NT])
        prob = sb("prob", [P, 2, NT])
        step_k = sb("step_k", [1, E, MAXT])
        t_cnt = sb("t_cnt", [1, E])
        t_gt = sb("t_gt", [1, E, MAXT])
        t_nt = sb("t_nt", [1, E])
        upto = sb("upto", [1, E, E])
        t_m = sb("t_m", [1, E, E])
        t_end = sb("t_end", [1, E])
        t_idx = sb("t_idx", [1, NTILE, E])
        t_ge = sb("t_ge", [1, NTILE, E])
        t_gn = sb("t_gn", [1, NTILE, E])
        t_e = sb("t_e", [1, NTILE])
        t_s = sb("t_s", [1, NTILE])
        t_o = sb("t_o", [1, NTILE])
        table = sb("table", [1, 2, NTILE], I32)
        tail = sb("tail", [1, E], I32)
        slot = [sb(f"slot{i}", [P, J, ROW]) for i in range(4)]
        wcur = [sb(f"wcur{i}", [P, WROW]) for i in range(2)]
        xeT = [sb(f"xeT{i}", [P, TILE]) for i in range(2)]
        hT = [sb(f"hT{i}", [P, HC, TILE]) for i in range(2)]
        ye = [sb(f"ye{i}", [P, J, D]) for i in range(2)]
        goes = [sb(f"goes{i}", [P, J], I32) for i in range(2)]
        F1raw = adj_in[0][:, :, :].rearrange("p a n -> p (a n)").rearrange("p (c d) -> p c d", d=D)
        F2raw = adj_in[1][:, :, :].rearrange("p a n -> p (a n)").rearrange("p (e h) -> p e h", h=H)
        Yin = [adj_in[i][:, 0:2, :].rearrange("p k (t d) -> p k t d", d=D) for i in range(2)]

        def bank(name):
            return ctx.enter_context(nc.psum_tensor(name, [P, 512], FP32))
        ps_t = [bank(f"ps_t{i}") for i in range(2)]
        ps_agg = bank("ps_agg")
        ps_h = [bank(f"ps_h{i}") for i in range(2)]
        ps_y = bank("ps_y")
        ps_x = bank("ps_x")
        ps_g = bank("ps_g")

        s_x0 = sem("x0_in")
        s_xr = sem("x_rest_in")
        s_adj = [sem(f"adj_in_sem{i}") for i in range(2)]
        s_const = sem("const_in")
        s_F1 = sem("F1_in")
        s_F2 = sem("F2_in")
        s_fb2 = sem("fb2_in")
        s_ident = sem("ident_ready")
        s_made = sem("constants_made")
        s_smallT = sem("small_transposed")
        s_smallc = sem("small_copied")
        s_epsid = sem("eps_ident_ready")
        s_epsadd = sem("eps_added")
        s_tp = sem("adj_transposed")
        s_evA = sem("adjT_even_ready")
        s_evD = sem("adjT_odd_ready")
        s_mm = sem("adj_product_done")
        s_xn = sem("xn_ready")
        s_agg = sem("aggT_ready")
        s_h = sem("h_done")
        s_hb = sem("hb_ready")
        s_ss = sem("squares_summed")
        s_rms = sem("rms_rstd_ready")
        s_hn = sem("hn_ready")
        s_hT = sem("hn_transposed")
        s_silu = sem("silu_ready")
        s_y = sem("y_done")
        s_x1 = sem("x1_ready")
        s_xb = sem("x_plus_b2_ready")
        s_mv1 = sem("ln1_stats_ready")
        s_rs1 = sem("ln1_rstd_ready")
        s_mv2 = sem("ln2_stats_ready")
        s_rs2 = sem("ln2_rstd_ready")
        s_row1 = sem("rows_first_ready")
        s_row2 = sem("rows_second_ready")
        s_xT = sem("xn2_transposed")
        s_xTc = sem("xn2T_ready")
        s_gate = sem("gate_done")
        s_both = sem("choices_ready")
        s_rank = sem("ranks_done")
        s_base = sem("base_updated")
        s_dest = sem("dest_ready")
        s_scat = [sem(f"rows_scattered{i}") for i in range(2)]
        s_dve = sem("dve_order")
        s_act = sem("act_order")
        s_pool = sem("pool_order")
        s_turn = sem("pool_turns")
        s_spare = sem("spare_rows_filled")
        s_tails = sem("tails_filled")
        s_table = sem("table_ready")
        s_wT = sem("weights_transposed")
        s_wTa = sem("weights_copied_act")
        s_wTd = sem("weights_copied_dve")
        s_fb1c = sem("fb1_copied")
        s_slot = [sem(f"slot_in{i}") for i in range(4)]
        s_wcur = [sem(f"wcur_in{i}") for i in range(2)]
        s_eT = sem("tile_transposed")
        s_eTc = sem("xeT_ready")
        s_goes = sem("goes_ready")
        s_l1 = sem("layer1_done")
        s_reluA = sem("relu_even_ready")
        s_reluD = sem("relu_odd_ready")
        s_l2 = sem("layer2_done")
        s_ye = sem("ye_ready")
        s_ysc = [sem(f"results_scattered{i}") for i in range(2)]
        s_exp = sem("exp_ready")
        s_yin = [sem(f"results_in{i}") for i in range(2)]
        s_out = sem("out_ready")
        s_stored = sem("out_stored")

        adj_g = adj.rearrange("b (h t p) m -> (b h) p t m", h=GPB, p=P)
        x_t = x.rearrange("b (t p) d -> p (b t) d", p=P)
        out_t = out.rearrange("b (t p) d -> p (b t) d", p=P)
        y_t = pairs_out.rearrange("(k t p) d -> p k t d", k=2, p=P)

        def wait(eng, s, v):
            if not (isinstance(v, int) and v <= 0):
                eng.wait_ge(s, v)

        class Order:

            def __init__(self, eng, s, links):
                self.eng, self.s, self.links, self.base, self.k = eng, s, links, 0, 0

            def step(self, base):
                self.base, self.k = base, 0

            def link(self, ins):
                self.k += 1
                ins.then_inc(self.s, 1)
                self.eng.wait_ge(self.s, self.base + self.k)

            def end(self):
                assert self.k <= self.links, self.k
                if self.k < self.links:
                    self.eng.sem_inc(self.s, self.links - self.k)

        def first_part(eng, step, last):
            def peeled(g):
                step(g, g % 2, g // 2)
            for g in range(4):
                peeled(g)
            with eng.Fori(2, B - 1) as b:
                for par in range(2):
                    step(b * 2 + par, par, b)
            for g in range(NG - 2, last + 1):
                peeled(g)

        def has(g, lag):
            return not isinstance(g, int) or 0 <= g - lag < NG

        LOOPED = (NTILE - 4) // 4

        def second_part(eng, step, lag):
            for t in range(4):
                step(t, t)
            with eng.Fori(1, 1 + LOOPED) as i:
                for k in range(4):
                    step(i * 4 + k, k)
            for t in range(4 + 4 * LOOPED, NTILE + lag):
                step(t, t % 4)

        def live(t, lag):
            return not isinstance(t, int) or 0 <= t - lag < NTILE

        def turn(t, k, n):
            return (t - k % n) // n if isinstance(t, int) else None

        block = ctx.enter_context(nc.Block())

        @block.sync
        def _(sp):
            sp.dma_start(x_all[:, 0:TPB, :], x_t[:, 0:TPB, :]).then_inc(s_x0, 16)
            sp.dma_start(adj_in[0][:, :, :], adj_g[0]).then_inc(s_adj[0], 16)
            sp.dma_start(adj_in[1][:, :, :], adj_g[1]).then_inc(s_adj[1], 16)
            sp.dma_start(x_all[:, TPB:NT, :], x_t[:, TPB:NT, :]).then_inc(s_xr, 16)
            with sp.Fori(1, B) as b:
                for par in range(2):
                    sp.wait_ge(s_tp, b * (2 * TPB) + (par - 1) * TPB)
                    sp.dma_start(adj_in[par][:, :, :],
                                 adj_g[bass.ds(b * 2 + par, 1)].rearrange("o p t m -> (o p) t m")
                                 ).then_inc(s_adj[par], 16)
            sp.wait_ge(s_tp, TPB * (NG - 1))
            sp.dma_start(F1raw, F1.rearrange("e (c p) d -> p (e c) d", p=P)).then_inc(s_F1, 16)
            sp.wait_ge(s_tp, TPB * NG)
            sp.dma_start(F2raw, F2.rearrange("e d h -> d e h")).then_inc(s_F2, 16)

            sp.wait_ge(s_table, 1)
            for e in range(E):
                row = sp.value_load(tail[0:1, e:e + 1], min_val=e * R, max_val=e * R + TOK)
                sp.dma_start(slots[bass.ds(row, TILE), :].rearrange("(p j) c -> p j c", j=J),
                             pad_rows[:, :, :]).then_inc(s_tails, 16)
            sp.wait_ge(s_tails, 16 * E)
            sp.wait_ge(s_spare, 16 * SPARE)
            sp.wait_ge(s_scat[0], 16 * GT * NG)
            sp.wait_ge(s_scat[1], 16 * GT * NG)
            sp.wait_ge(s_wTa, E)
            sp.wait_ge(s_wTd, E)
            sp.wait_ge(s_fb1c, 1)
            sp.wait_ge(s_fb2, 16)

            def load(t, k):
                expert = sp.value_load(table[0:1, 0, bass.ds(t, 1)], min_val=0, max_val=E - 1)
                first = sp.value_load(table[0:1, 1, bass.ds(t, 1)], min_val=0,
                                      max_val=E * R + (SPARE - 1) * TILE)
                wait(sp, s_eT, t - 3)
                wait(sp, s_goes, t - 3)
                sp.dma_start(slot[k][:, :, :], slots[bass.ds(first, TILE), :]
                             .rearrange("(p j) c -> p j c", j=J)).then_inc(s_slot[k], 16)
                wait(sp, s_l2, t - 1)
                wait(sp, s_ye, t - 1)
                sp.dma_start(wcur[k % 2][:, :],
                             weights[:, bass.ds(expert, 1), :].rearrange("p o w -> p (o w)")
                             ).then_inc(s_wcur[k % 2], 16)
            second_part(sp, load, 0)

            for b in range(B):
                if b == 0:
                    for k in range(2):
                        n = (NTILE + 1 - k) // 2
                        sp.wait_ge(s_ysc[k], 16 * J * n)
                if b >= 2:
                    sp.wait_ge(s_out, b - 1)
                for c in range(2):
                    sp.dma_start(Yin[b % 2][:, c, :, :], y_t[:, c, b * TPB:(b + 1) * TPB, :]).then_inc(s_yin[b % 2], 16)

        @block.tensor
        def _(pe):
            pe.wait_ge(s_const, 16 * 10)
            pe.wait_ge(s_ident, 1)
            pe.transpose(ps_g[:, 0:NS], small[:, :], ident[0:NS, 0:NS]).then_inc(s_smallT, 1)

            def step(g, par, b):
                def T(m):
                    if m == 0:
                        pe.wait_ge(s_epsadd, 4 * g + 4)
                    wait(pe, s_evD if m % 2 else s_evA, 4 * g + m // 2)
                    for j in range(GT):
                        ins = pe.transpose(ps_t[m % 2][:, j * P:(j + 1) * P],
                                           adj_in[par][:, j, m * P:(m + 1) * P], ident[:, :])
                    ins.then_inc(s_tp, 1)

                def M(m):
                    if m == 0:
                        if par == 0:
                            pe.wait_ge(s_xn, b + 1)
                        wait(pe, s_agg, g)
                    pe.wait_ge(s_evD if m % 2 else s_evA, 4 * g + m // 2 + 1)
                    pe.matmul(ps_agg[:, :], xn[:, m, :], adjT[:, m % 4, :],
                              start=(m == 0), stop=(m == TPB - 1)).then_inc(s_mm, 1)

                def tm(m):
                    if has(g, 0):
                        T(m)
                        if m >= 1:
                            M(m - 1)

                tm(0)
                tm(1)
                tm(2)
                if has(g, 2):
                    q = g - 2
                    pe.wait_ge(s_row1, q + 1)
                    for j in range(GT):
                        ins = pe.transpose(ps_x[:, j * P:(j + 1) * P], rows[par][:, 0, j, 0:D], ident[:, :])
                    ins.then_inc(s_xT, 1)
                if has(g, 1):
                    q = g - 1
                    pe.wait_ge(s_agg, q + 1)
                    for j in range(GT):
                        if j < 2:
                            wait(pe, s_silu, 4 * q - 1 + j)
                        else:
                            pe.wait_ge(s_hb, 4 * q + j - 1)
                        pe.matmul(ps_h[j % 2][:, :], aggT[1 - par][:, j * P:(j + 1) * P], W1s[:, :],
                                  start=True, stop=True).then_inc(s_h, 1)
                tm(3)
                if has(g, 2):
                    q = g - 2
                    pe.wait_ge(s_xTc, q + 1)
                    if isinstance(q, int) and q == 0:
                        pe.wait_ge(s_smallc, 1)
                    wait(pe, s_base, q)
                    for j in range(GT):
                        ins = pe.matmul(ps_g[:, j * E:(j + 1) * E], xn2T[:, j * P:(j + 1) * P], WgT,
                                        start=True, stop=True)
                    ins.then_inc(s_gate, 1)
                tm(4)
                tm(5)
                if has(g, 1):
                    q = g - 1
                    pe.wait_ge(s_hn, q + 1)
                    for c in range(HC):
                        if c >= 2:
                            pe.wait_ge(s_silu, 4 * q + c - 1)
                        for j in range(GT):
                            ins = pe.transpose(ps_h[c % 2][:, j * P:(j + 1) * P],
                                               hn[:, j, c * P:(c + 1) * P], ident[:, :])
                        ins.then_inc(s_hT, 1)
                tm(6)
                if has(g, 2):
                    q = g - 2
                    pe.wait_ge(s_both, q + 1)
                    pe.matmul(ps_g[:, 0:(GT + 1) * E], earlier[:, :],
                              both[:, :, :].rearrange("p t e -> p (t e)"), start=True, stop=False)
                    for j in range(GT):
                        n = GT - j
                        ins = pe.matmul(ps_g[:, (j + 1) * E:(GT + 1) * E].rearrange("p (n e) -> p n e", e=E),
                                        ones[:, :], both[:, j:j + 1, :].broadcast_to([P, n, E]),
                                        start=False, stop=(j == GT - 1))
                    ins.then_inc(s_rank, 1)
                tm(7)
                if has(g, 1):
                    q = g - 1
                    pe.wait_ge(s_silu, 4 * q + 4)
                    wait(pe, s_x1, q)
                    for j in range(GT):
                        for c in range(HC):
                            ins = pe.matmul(ps_y[:, j * P:(j + 1) * P], siluT[:, c, j * P:(j + 1) * P],
                                            W2s[:, c, :], start=(c == 0), stop=(c == HC - 1))
                    ins.then_inc(s_y, 1)
                if has(g, 0):
                    M(TPB - 1)
            first_part(pe, step, NG + 1)

            pe.wait_ge(s_F1, 16)
            pe.wait_ge(s_F2, 16)
            for e in range(E):
                if e == 0:
                    pe.wait_ge(s_evA, 4 * NG)
                    pe.wait_ge(s_evD, 4 * NG)
                wait(pe, s_wTa, e)
                for c in range(HC):
                    ins = pe.transpose(ps_t[0][:, c * P:(c + 1) * P], F1raw[:, e * HC + c, :], ident[:, :])
                ins.then_inc(s_wT, 1)
                wait(pe, s_wTd, e)
                for c in range(HC):
                    ins = pe.transpose(ps_t[1][:, c * P:(c + 1) * P], F2raw[:, e, c * P:(c + 1) * P], ident[:, :])
                ins.then_inc(s_wT, 1)

            ps_e = [ps_t[0], ps_t[1]]
            ps_1 = [ps_agg, ps_h[0], ps_h[1], ps_x]
            ps_2 = [ps_y, ps_g]

            def tile(t, k):
                if live(t, 0):
                    pe.wait_ge(s_slot[k], 16 * (t // 4 + 1) if isinstance(t, int) else t * 4 + (16 - 4 * k))
                    wait(pe, s_eTc, t - 1)
                    for j in range(J):
                        ins = pe.transpose(ps_e[k % 2][:, j * P:(j + 1) * P], slot[k][:, j, 0:D], ident[:, :])
                    ins.then_inc(s_eT, 1)
                if live(t, 1):
                    u, ku = t - 1, (k - 1) % 4
                    pe.wait_ge(s_eTc, u + 1)
                    pe.wait_ge(s_wcur[ku % 2],
                               16 * (u // 2 + 1) if isinstance(u, int) else u * 8 + (16 - 8 * (ku % 2)))
                    for c in range(HC):
                        wait(pe, s_reluD if c % 2 else s_reluA, 2 * (u - 1) + c // 2 + 1)
                        pe.matmul(ps_1[c][:, 0:TILE], wcur[ku % 2][:, CW1 + c * P:CW1 + (c + 1) * P],
                                  xeT[ku % 2][:, :], start=True, stop=True).then_inc(s_l1, 1)
                if live(t, 2):
                    u, ku = t - 2, (k - 2) % 4
                    pe.wait_ge(s_reluA, 2 * u + 2)
                    pe.wait_ge(s_reluD, 2 * u + 2)
                    wait(pe, s_ye, u - 1)
                    for j in range(J):
                        for c in range(HC):
                            ins = pe.matmul(ps_2[ku % 2][:, j * P:(j + 1) * P], hT[ku % 2][:, c, j * P:(j + 1) * P],
                                            wcur[ku % 2][:, CW2 + c * D:CW2 + (c + 1) * D],
                                            start=(c == 0), stop=(c == HC - 1))
                    ins.then_inc(s_l2, 1)
            second_part(pe, tile, 2)

        @block.scalar
        def _(act):
            act.dma_start(small[0:HC, :], rms_w.rearrange("(c p) -> c p", p=P)).then_inc(s_const, 16)
            act.dma_start(small[HC:HC + E * HC, :], fb1.rearrange("e (c p) -> (e c) p", p=P)).then_inc(s_const, 16)
            act.dma_start(small[HC + E * HC:NS, :], Wg[:, :]).then_inc(s_const, 16)
            act.dma_start(epss[:, :], eps.to_broadcast([P, 1])).then_inc(s_const, 16)
            act.dma_start(W1s[:, :], W1[:, :]).then_inc(s_const, 16)
            act.dma_start(b1s[:, :], b1[None, :].to_broadcast([P, H])).then_inc(s_const, 16)
            act.dma_start(b2s[:, :], b2[None, :].to_broadcast([P, D])).then_inc(s_const, 16)
            act.dma_start(bgs[:, :], bg[None, :].to_broadcast([P, E])).then_inc(s_const, 16)
            act.dma_start(W2s[:, 0:2, :], W2[0:H // 2, :].rearrange("(c p) d -> p c d", p=P)).then_inc(s_const, 16)
            act.dma_start(W2s[:, 2:4, :], W2[H // 2:H, :].rearrange("(c p) d -> p c d", p=P)).then_inc(s_const, 16)
            act.dma_start(weights[:, :, CB2:CB2 + D], fb2[None, :, :].to_broadcast([P, E, D])).then_inc(s_fb2, 16)

            def step(g, par, b):
                def evac(m):
                    if has(g, 0):
                        act.wait_ge(s_tp, TPB * g + m + 1)
                        wait(act, s_mm, TPB * g + m - 3)
                        act.activation(adjT[:, m % 4, :], ps_t[m % 2][:, :], ACT.Copy).then_inc(s_evA, 1)
                evac(0)
                evac(2)
                if has(g, 2):
                    q = g - 2
                    act.wait_ge(s_xT, q + 1)
                    wait(act, s_gate, q)
                    act.activation(xn2T[:, :], ps_x[:, :], ACT.Copy).then_inc(s_xTc, 1)
                    act.wait_ge(s_row1, q + 1)
                    act.activation(rows[par][:, 1, :, 0:D], rows[par][:, 0, :, 0:D], ACT.Copy).then_inc(s_row2, 1)
                if has(g, 1):
                    q = g - 1
                    wait(act, s_rms, q)
                    wait(act, s_hT, 4 * q)
                    for j in range(GT):
                        act.wait_ge(s_hb, 4 * q + j + 1)
                        act.activation(hn[:, j, :], hb[:, j, :], ACT.Square,
                                       accum_out=ss[:, j:j + 1]).then_inc(s_ss, 1)
                evac(4)
                if has(g, 1):
                    q = g - 1
                    wait(act, s_y, q)
                    for c in range(HC):
                        act.wait_ge(s_hT, 4 * q + c + 1)
                        act.activation(siluT[:, c, :], ps_h[c % 2][:, :], ACT.Silu,
                                       scale=rmsT[:, c:c + 1]).then_inc(s_silu, 1)
                evac(6)
            act.wait_ge(s_smallc, 1)
            act.activation(weights[:, :, CB1:CB1 + HC], fb1T.rearrange("p (e c) -> p e c", c=HC),
                           ACT.Copy).then_inc(s_fb1c, 1)
            first_part(act, step, NG + 1)

            for e in range(E):
                act.wait_ge(s_wT, 2 * e + 1)
                act.activation(weights[:, e, CW1:CW1 + H], ps_t[0][:, :], ACT.Copy).then_inc(s_wTa, 1)

            ps_1 = [ps_agg, ps_h[0], ps_h[1], ps_x]

            def tile(t, k):
                if live(t, 1):
                    u, ku = t - 1, (k - 1) % 4
                    for c in (0, 2):
                        act.wait_ge(s_l1, 4 * u + c + 1)
                        wait(act, s_l2, u - 1)
                        act.activation(hT[ku % 2][:, c, :], ps_1[c][:, 0:TILE], ACT.Relu,
                                       bias=wcur[ku % 2][:, CB1 + c:CB1 + c + 1]).then_inc(s_reluA, 1)
            second_part(act, tile, 1)

            act.wait_ge(s_base, NG)
            act.activation(prob[:, 1, :], gap[:, :], ACT.Exp).then_inc(s_exp, 1)
            for b in range(B):
                act.wait_ge(s_out, b + 1)
                act.dma_start(out_t[:, b * TPB:(b + 1) * TPB, :],
                              x_all[:, b * TPB:(b + 1) * TPB, :]).then_inc(s_stored, 16)
            act.wait_ge(s_stored, 16 * B)

        @block.gpsimd
        def _(pool):
            order = Order(pool, s_pool, 4)
            order.step(0)
            pool.memset(ident[:, :], 0.0)
            pool.memset(minus_half[:, :], -0.5)
            pool.memset(ln_eps[:, :], 1e-5)
            pool.memset(rms_eps[:, :], 1e-6 * H)
            pool.memset(earlier[:, :], 1.0)
            pool.memset(pad_rows[:, :, :], 0.0)
            order.link(pool.memset(ones[:, :], 1.0))
            pool.affine_select(out=ident[:, :], in_=ident[:, :], compare_op=ALU.not_equal, fill=1.0, base=0,
                               pattern=[[-1, P]], channel_multiplier=1).then_inc(s_ident, 1)
            pool.affine_select(out=earlier[:, :], in_=earlier[:, :], compare_op=ALU.is_gt, fill=0.0, base=0,
                               pattern=[[1, P]], channel_multiplier=-1)
            pool.iota(place_id[:, :, :], [[TOK, 2], [P, NT]], base=0, channel_multiplier=1,
                      allow_small_or_imprecise_dtypes=True)
            pool.iota(falling[:, :, :], [[0, GT], [-1, E]], base=E, channel_multiplier=0,
                      allow_small_or_imprecise_dtypes=True)
            pool.iota(base0[:, :], [[R, E]], base=0, channel_multiplier=0, allow_small_or_imprecise_dtypes=True)
            pool.iota(step_k[:, :, :], [[0, E], [TILE, MAXT]], base=0, channel_multiplier=0,
                      allow_small_or_imprecise_dtypes=True)
            pool.iota(t_idx[:, :, :], [[1, NTILE], [0, E]], base=0, channel_multiplier=0,
                      allow_small_or_imprecise_dtypes=True)
            pool.iota(upto[:, :, :], [[1, E], [-1, E]], base=0, channel_multiplier=0,
                      allow_small_or_imprecise_dtypes=True)
            order.link(pool.memset(pad_rows[:, :, D:D + 1], NOWHERE))
            pool.memset(both_pad := both[:, GT:GT + 1, :], 0.0).then_inc(s_made, 1)
            pool.wait_ge(s_const, 16 * 10)
            order.link(pool.tensor_scalar(eps_ident[:, :], ident[:, :], epss[:, 0:1], 1.0, ALU.mult, ALU.mult))
            for n in range(SPARE):
                r = E * R + n * TILE
                pool.dma_start(slots[r:r + TILE, :].rearrange("(p j) c -> p j c", j=J),
                               pad_rows[:, :, :]).then_inc(s_spare, 16)

            def inv_sqrt(square_, eps_, scratch, result, n, s_done):
                order.link(pool.tensor_tensor(scratch, square_, eps_[:, 0:n], ALU.add))
                pool.tensor_tensor(result, scratch, minus_half[:, 0:n], ALU.pow).then_inc(s_done, 1)

            def add_eps(g, par, b):
                pool.wait_ge(s_adj[par], 16 * b + 16)
                for j in range(GT):
                    col = (par * GT + j) * P
                    pool.tensor_tensor(adj_in[par][:, j, col:col + P], adj_in[par][:, j, col:col + P],
                                       eps_ident[:, :], ALU.add).then_inc(s_epsadd, 1)

            def x_plus_b2(b):
                xv = x_all[:, bass.ds(b * TPB, TPB), :] if not isinstance(b, int) else x_all[:, b * TPB:(b + 1) * TPB, :]
                pool.tensor_tensor(xv, xv, b2s[:, None, :].broadcast_to([P, TPB, D]), ALU.add).then_inc(s_xb, 1)

            pool.wait_ge(s_mv1, 1)
            inv_sqrt(mv1[:, :, 1], ln_eps, ve1[:, :], rstd1[:, :], TPB, s_rs1)
            add_eps(0, 0, 0)
            order.end()

            def step(g, par, b):
                order.step((g + 1) * 4)
                if has(g, 3):
                    pool.wait_ge(s_dest, g - 2)
                    pool.wait_ge(s_row2, g - 2)
                if has(g, 1):
                    q = g - 1
                    pool.wait_ge(s_ss, 4 * q + 4)
                    wait(pool, s_hn, q)
                    inv_sqrt(ss[:, :], rms_eps, rms_var[:, :], rms_rstd[:, :], GT, s_rms)
                if has(g, -1):
                    add_eps(g + 1, 1 - par, b + par)
                if par == 0 and has(g, 0):
                    pool.wait_ge(s_xn, b + 1)
                    pool.sem_inc(s_turn, 1)
                    x_plus_b2(b)
                if has(g, 3):
                    for c in range(2):
                        for j in range(GT):
                            pool.indirect_dma_start(
                                out=slots, out_offset=bass.IndirectOffsetOnAxis(ap=dest[1 - par][:, c, j:j + 1], axis=0),
                                in_=rows[1 - par][:, c, j, :], in_offset=None,
                                bounds_check=E * R - 1, oob_is_err=True).then_inc(s_scat[1 - par], 16)
                if par == 1 and has(g, -1):
                    pool.wait_ge(s_mv1, b + 2)
                    inv_sqrt(mv1[:, :, 1], ln_eps, ve1[:, :], rstd1[:, :], TPB, s_rs1)
                if has(g, 1):
                    q = g - 1
                    pool.wait_ge(s_mv2, q + 1)
                    wait(pool, s_row1, q)
                    inv_sqrt(mv2[:, :, 1], ln_eps, ve2[:, :], rstd2[:, :], GT, s_rs2)
                order.end()
            first_part(pool, step, NG + 2)

            def scatter(t, k):
                if live(t, 2):
                    u, ku = t - 2, (k - 2) % 2
                    pool.wait_ge(s_ye, u + 1)
                    pool.sem_inc(s_turn, 1)
                    for j in range(J):
                        pool.indirect_dma_start(
                            out=pairs_out, out_offset=bass.IndirectOffsetOnAxis(ap=goes[ku][:, j:j + 1], axis=0),
                            in_=ye[ku][:, j, :], in_offset=None,
                            bounds_check=2 * TOK - 1, oob_is_err=False).then_inc(s_ysc[ku], 16)
            second_part(pool, scatter, 2)

        @block.vector
        def _(dve):
            order = Order(dve, s_dve, 21)
            order.step(0)

            def ln1_stats(b):
                for j in range(TPB):
                    t = b * TPB + j
                    src = x_all[:, t, :] if isinstance(b, int) else x_all[:, bass.ds(t, 1), :].rearrange("p o d -> p (o d)")
                    ins = dve.bn_stats(st1[:, j, :], src)
                order.link(ins)
                wait(dve, s_rs1, b)

            def ln1_aggregate(b):
                for j in range(TPB):
                    ins = dve.bn_aggr(mv1[:, j, :], st1[:, j, :])
                ins.then_inc(s_mv1, 1)

            def ln1_norm(b):
                dve.wait_ge(s_rs1, b + 1)
                for j in range(TPB):
                    t = b * TPB + j
                    src = x_all[:, t, :] if isinstance(b, int) else x_all[:, bass.ds(t, 1), :].rearrange("p o d -> p (o d)")
                    ins = dve.tensor_scalar(xn[:, j, :], src, mv1[:, j, 0:1], rstd1[:, j:j + 1],
                                            ALU.subtract, ALU.mult)
                ins.then_inc(s_xn, 1)

            dve.wait_ge(s_x0, 16)
            ln1_stats(0)
            ln1_aggregate(0)
            dve.wait_ge(s_made, 1)
            dve.tensor_copy(base[:, :], base0[:, :])
            dve.tensor_scalar(upto[:, :, :], upto[:, :, :], 0.0, None, ALU.is_ge)
            dve.wait_ge(s_smallT, 1)
            dve.tensor_copy(smallT[:, :], ps_g[:, 0:NS]).then_inc(s_smallc, 1)
            ln1_norm(0)
            order.end()

            def step(g, par, b):
                order.step((g + 1) * 21)

                def evac(m):
                    if has(g, 0):
                        dve.wait_ge(s_tp, TPB * g + m + 1)
                        wait(dve, s_mm, TPB * g + m - 3)
                        dve.tensor_copy(adjT[:, m % 4, :], ps_t[m % 2][:, :]).then_inc(s_evD, 1)
                evac(1)
                if has(g, 1):
                    q = g - 1
                    for j in range(GT):
                        dve.wait_ge(s_h, 4 * q + j + 1)
                        dve.tensor_tensor(hb[:, j, :], ps_h[j % 2][:, :], b1s[:, :], ALU.add).then_inc(s_hb, 1)
                evac(3)
                if has(g, 1):
                    q = g - 1
                    dve.wait_ge(s_rms, q + 1)
                    wait(dve, s_hT, 4 * q)
                    for j in range(GT):
                        ins = dve.tensor_scalar(hn[:, j, :], hb[:, j, :], rms_rstd[:, j:j + 1], float(H) ** 0.5,
                                                ALU.mult, ALU.mult)
                    ins.then_inc(s_hn, 1)
                evac(5)
                if has(g, 2):
                    q = g - 2
                    dve.wait_ge(s_gate, q + 1)
                    order.link(dve.tensor_tensor(score[:, :, :], ps_g[:, 0:GT * E].rearrange("p (t e) -> p t e", e=E),
                                                 bgs[:, None, :].broadcast_to([P, GT, E]), ALU.add))
                    src = score
                    for c in range(2):
                        order.link(dve.reduce_max(top[:, c, :], src[:, :, :], AX.X))
                        order.link(dve.tensor_tensor(tied[:, :, :], src[:, :, :],
                                                     top[:, c, :, None].broadcast_to([P, GT, E]), ALU.is_equal))
                        order.link(dve.tensor_tensor(tied[:, :, :], tied[:, :, :], falling[:, :, :], ALU.mult))
                        order.link(dve.reduce_max(first_of[:, c, :], tied[:, :, :], AX.X))
                        order.link(dve.tensor_tensor(onehot[:, c, :, :], falling[:, :, :],
                                                     first_of[:, c, :, None].broadcast_to([P, GT, E]), ALU.is_equal))
                        if c == 0:
                            order.link(dve.scalar_tensor_tensor(rest[:, :, :], onehot[:, 0, :, :], -BIG, score[:, :, :],
                                                                ALU.mult, ALU.add))
                            src = rest
                    dve.tensor_tensor(both[:, 0:GT, :], onehot[:, 0, :, :], onehot[:, 1, :, :], ALU.add).then_inc(s_both, 1)
                    gv = gap[:, q * GT:(q + 1) * GT] if isinstance(q, int) else gap[:, bass.ds(q * GT, GT)]
                    order.link(dve.tensor_tensor(gv, top[:, 1, :], top[:, 0, :], ALU.subtract))
                if par == 1 and has(g, -1):
                    if isinstance(b, int) and b == 0:
                        dve.wait_ge(s_xr, 16)
                    ln1_stats(b + 1)
                evac(7)
                if par == 1 and has(g, -1):
                    ln1_aggregate(b + 1)
                if has(g, 2):
                    q = g - 2
                    dve.wait_ge(s_rank, q + 1)
                    order.link(dve.tensor_tensor(place[:, :, :], ps_g[:, 0:GT * E].rearrange("p (t e) -> p t e", e=E),
                                                 base[:, None, :].broadcast_to([P, GT, E]), ALU.add))
                    dve.tensor_tensor(base[:, :], base[:, :], ps_g[:, GT * E:(GT + 1) * E], ALU.add).then_inc(s_base, 1)
                    order.link(dve.tensor_tensor(picked[:, :, :, :], onehot[:, :, :, :],
                                                 place[:, None, :, :].broadcast_to([P, 2, GT, E]), ALU.mult))
                    wait(dve, s_scat[par], (q // 2) * 128 if isinstance(q, int) else (q - par) * 64)
                    with nc.allow_low_precision(reason="sums of whole numbers below 2**24, one of them not zero"):
                        dve.tensor_reduce(dest[par][:, :, :].rearrange("p c t -> p (c t)"),
                                          picked[:, :, :, :].rearrange("p c t e -> p (c t) e"),
                                          AX.X, ALU.add).then_inc(s_dest, 1)
                if has(g, 1):
                    q = g - 1
                    dve.wait_ge(s_y, q + 1)
                    dve.wait_ge(s_xb, b + par)
                    xv = x_all[:, q * GT:(q + 1) * GT, :] if isinstance(q, int) else x_all[:, bass.ds(q * GT, GT), :]
                    ins = dve.tensor_tensor(xv, ps_y[:, :].rearrange("p (t d) -> p t d", d=D), xv, ALU.add)
                    order.k += 1
                    ins.then_inc(s_x1, 1)
                    order.k -= 1
                if has(g, 1):
                    dve.wait_ge(s_x1, g)
                if has(g, 0):
                    dve.wait_ge(s_mm, TPB * g + TPB)
                    wait(dve, s_h, 4 * (g - 1))
                    dve.tensor_copy(aggT[par][:, :], ps_agg[:, :]).then_inc(s_agg, 1)
                if par == 1 and has(g, -1):
                    ln1_norm(b + 1)
                if has(g, 1):
                    q = g - 1
                    def tok(j):
                        t = q * GT + j
                        return x_all[:, t, :] if isinstance(q, int) else x_all[:, bass.ds(t, 1), :].rearrange("p o d -> p (o d)")
                    for j in range(GT):
                        ins = dve.bn_stats(st2[:, j, :], tok(j))
                    order.link(ins)
                    wait(dve, s_scat[1 - par], (q // 2) * 128 if isinstance(q, int) else (q - (1 - par)) * 64)
                    pv = place_id[:, :, q * GT:(q + 1) * GT] if isinstance(q, int) else place_id[:, :, bass.ds(q * GT, GT)]
                    dve.tensor_copy(rows[1 - par][:, :, :, D], pv)
                    for j in range(GT):
                        ins = dve.bn_aggr(mv2[:, j, :], st2[:, j, :])
                    ins.then_inc(s_mv2, 1)
                    dve.wait_ge(s_rs2, q + 1)
                    for j in range(GT):
                        ins = dve.tensor_scalar(rows[1 - par][:, 0, j, 0:D], tok(j), mv2[:, j, 0:1], rstd2[:, j:j + 1],
                                                ALU.subtract, ALU.mult)
                    ins.then_inc(s_row1, 1)
                order.end()
            first_part(dve, step, NG + 1)

            order.step((NG + 3) * 21)
            dve.wait_ge(s_base, NG)
            dve.tensor_copy(tail[:, :], base[0:1, :])
            order.link(dve.tensor_tensor(t_cnt[:, :], base[0:1, :], base0[0:1, :], ALU.subtract))
            order.link(dve.tensor_tensor(t_gt[:, :, :], t_cnt[:, :, None].broadcast_to([1, E, MAXT]), step_k[:, :, :], ALU.is_gt))
            order.link(dve.tensor_reduce(t_nt[:, :], t_gt[:, :, :], AX.X, ALU.add))
            order.link(dve.tensor_tensor(t_m[:, :, :], t_nt[:, None, :].broadcast_to([1, E, E]), upto[:, :, :], ALU.mult))
            order.link(dve.tensor_reduce(t_end[:, :], t_m[:, :, :], AX.X, ALU.add))
            order.link(dve.tensor_tensor(t_ge[:, :, :], t_idx[:, :, :], t_end[:, None, :].broadcast_to([1, NTILE, E]), ALU.is_ge))
            order.link(dve.tensor_tensor(t_gn[:, :, :], t_ge[:, :, :], t_nt[:, None, :].broadcast_to([1, NTILE, E]), ALU.mult))
            dve.tensor_reduce(t_e[:, :], t_ge[:, :, :], AX.X, ALU.add)
            order.link(dve.tensor_reduce(t_s[:, :], t_gn[:, :, :], AX.X, ALU.add))
            order.link(dve.tensor_tensor(t_o[:, :], t_idx[:, :, 0], t_s[:, :], ALU.subtract))
            order.link(dve.tensor_scalar(t_o[:, :], t_o[:, :], float(TILE), None, ALU.mult))
            dve.scalar_tensor_tensor(table[:, 1, :], t_e[:, :], float(R), t_o[:, :], ALU.mult, ALU.add)
            dve.tensor_scalar(table[:, 0, :], t_e[:, :], float(E - 1), None, ALU.min).then_inc(s_table, 1)
            order.end()

            for e in range(E):
                dve.wait_ge(s_wT, 2 * e + 2)
                dve.tensor_copy(weights[:, e, CW2:CW2 + H], ps_t[1][:, :]).then_inc(s_wTd, 1)

            ps_e = [ps_t[0], ps_t[1]]
            ps_1 = [ps_agg, ps_h[0], ps_h[1], ps_x]
            ps_2 = [ps_y, ps_g]

            def tile(t, k):
                if live(t, 0):
                    dve.wait_ge(s_eT, t + 1)
                    wait(dve, s_l1, 4 * (t - 1))
                    dve.tensor_copy(xeT[k % 2][:, :], ps_e[k % 2][:, 0:TILE]).then_inc(s_eTc, 1)
                if live(t, 1):
                    u, ku = t - 1, (k - 1) % 4
                    for c in (1, 3):
                        dve.wait_ge(s_l1, 4 * u + c + 1)
                        wait(dve, s_l2, u - 1)
                        dve.tensor_scalar(hT[ku % 2][:, c, :], ps_1[c][:, 0:TILE],
                                          wcur[ku % 2][:, CB1 + c:CB1 + c + 1], 0.0,
                                          ALU.add, ALU.max).then_inc(s_reluD, 1)
                if live(t, 2):
                    u, ku = t - 2, (k - 2) % 4
                    dve.wait_ge(s_l2, u + 1)
                    wait(dve, s_ysc[ku % 2], (u // 2) * 16 * J if isinstance(u, int) else u * (8 * J) - (ku % 2) * 8 * J)
                    dve.tensor_copy(goes[ku % 2][:, :], slot[ku][:, :, D]).then_inc(s_goes, 1)
                    dve.tensor_tensor(ye[ku % 2][:, :, :], ps_2[ku % 2][:, 0:TILE].rearrange("p (j d) -> p j d", d=D),
                                      wcur[ku % 2][:, None, CB2:CB2 + D].broadcast_to([P, J, D]), ALU.add).then_inc(s_ye, 1)
            second_part(dve, tile, 2)

            order.step((NG + 4) * 21)
            dve.wait_ge(s_exp, 1)
            order.link(dve.tensor_scalar(prob[:, 0, :], prob[:, 1, :], 1.0, None, ALU.add))
            order.link(dve.reciprocal(prob[:, 0, :], prob[:, 0, :]))
            order.link(dve.tensor_tensor(prob[:, 1, :], prob[:, 1, :], prob[:, 0, :], ALU.mult))
            for b in range(B):
                dve.wait_ge(s_yin[b % 2], 32 * (b // 2 + 1))
                for c in range(2):
                    for j in range(TPB):
                        t = b * TPB + j
                        ins = dve.scalar_tensor_tensor(x_all[:, t, :], Yin[b % 2][:, c, j, :], prob[:, c, t:t + 1],
                                                       x_all[:, t, :], ALU.mult, ALU.add)
                    if c == 0:
                        order.link(ins)
                ins.then_inc(s_out, 1)


_INS = ["x", "adj", "L0_gnn_epsilon", "L0_gnn_W1", "L0_gnn_b1", "L0_gnn_rms_weight", "L0_gnn_W2", "L0_gnn_b2",
        "L0_ffn_Wg", "L0_ffn_bg", "L0_ffn_W1", "L0_ffn_b1", "L0_ffn_W2", "L0_ffn_b2"]


def kernel(**inputs):
    import concourse.bacc as bacc
    from concourse.bass_utils import run_bass_kernel_spmd

    nc = bacc.Bacc("TRN2", target_bir_lowering=False, num_devices=1)
    arrays, args = {}, []
    for name in _INS:
        a = np.ascontiguousarray(inputs[name])
        if a.ndim == 0:
            a = a.reshape(1, 1)
        arrays[f"in_{name}"] = a
        args.append(nc.dram_tensor(f"in_{name}", a.shape, mybir.dt.from_np(a.dtype), kind="ExternalInput").ap())
    shape = inputs["x"].shape
    args.append(nc.dram_tensor("out_0", shape, FP32, kind="ExternalOutput").ap())
    build(nc, *args)
    r = run_bass_kernel_spmd(nc, [arrays], core_ids=[0])
    return r.results[0]["out_0"]
```

```python
from contextlib import ExitStack

import numpy as np
import concourse.bass as bass
from concourse import mybir

FP32 = mybir.dt.float32
BF16 = mybir.dt.bfloat16
I32 = mybir.dt.int32
ALU = mybir.AluOpType
ACT = mybir.ActivationFunctionType
AX = mybir.AxisListType
P = 128
TILE = 384


def build(nc, x, adj, eps, W1, b1, rms_w, W2, b2, Wg, bg, F1, fb1, F2, fb2, out):
    B, N, D = x.shape
    H = W1.shape[1]
    E = Wg.shape[0]
    TOK = B * N
    NT = TOK // P
    TPB = N // P
    GT = 4
    GTOK = GT * P
    NG = NT // GT
    GPB = TPB // GT
    assert GPB == 2
    HC = H // P
    J = TILE // P
    NTILE = (2 * TOK + E * (TILE - 1)) // TILE
    MAXT = -(-TOK // TILE)
    R = TOK + TILE
    SPARE = NTILE - -(-2 * TOK // TILE)
    ID, GAP, CHOICE = D, D + 1, D + 2
    ROW = D + 3
    CW1, CB1, CW2, CB2 = 0, H, H + HC, H + HC + H
    WROW = CB2 + D
    BIG = 3.0e38

    slots = nc.dram_tensor("slots", [E * R + SPARE * TILE, ROW], FP32, kind="Internal").ap()

    ctx = ExitStack()
    with ctx:
        def sb(name, shape, dt=FP32):
            return ctx.enter_context(nc.sbuf_tensor(name, shape, dt))

        def sem(name):
            return ctx.enter_context(nc.semaphore(name))

        x_all = sb("x_all", [P, NT, D])
        adj_in = [sb(f"adj_in{i}", [P, GT, N]) for i in range(2)]
        adjT = sb("adjT", [P, 4, GTOK])
        xn = sb("xn", [P, TPB, D])
        aggT = [sb(f"aggT{i}", [P, GTOK]) for i in range(2)]
        hb = sb("hb", [P, GT, H])
        hn = sb("hn", [P, GT, H])
        siluT = sb("siluT", [P, HC, GTOK])
        rows = [sb(f"rows{i}", [P, 2, GT, ROW]) for i in range(2)]
        xn2T = sb("xn2T", [P, GTOK])
        weights = sb("weights", [P, E, WROW])
        W1s = sb("W1s", [P, H])
        W2s = sb("W2s", [P, HC, D])
        b1s = sb("b1s", [P, H])
        b2s = sb("b2s", [P, D])
        bgs = sb("bgs", [P, E])
        epss = sb("epss", [P, 1])
        NS = HC + E * HC + E
        small = sb("small", [NS, D])
        smallT = sb("smallT", [P, NS])
        rmsT, fb1T, WgT = smallT[:, 0:HC], smallT[:, HC:HC + E * HC], smallT[:, HC + E * HC:NS]
        ident = sb("ident", [P, P])
        eps_ident = sb("eps_ident", [P, P])
        earlier = sb("earlier", [P, P], BF16)
        ones = sb("ones", [P, P], BF16)
        minus_half = sb("minus_half", [P, TPB])
        ln_eps = sb("ln_eps", [P, TPB])
        rms_eps = sb("rms_eps", [P, TPB])
        falling = sb("falling", [P, GT, E])
        token_id = sb("token_id", [P, NT])
        pad_rows = sb("pad_rows", [P, J, ROW])
        ss = sb("ss", [P, GT])
        rms_var = sb("rms_var", [P, GT])
        rms_rstd = sb("rms_rstd", [P, GT])
        st1 = sb("st1", [P, TPB, 6])
        mv1 = sb("mv1", [P, TPB, 2])
        ve1 = sb("ve1", [P, TPB])
        rstd1 = sb("rstd1", [P, TPB])
        st2 = sb("st2", [P, GT, 6])
        mv2 = sb("mv2", [P, GT, 2])
        ve2 = sb("ve2", [P, GT])
        rstd2 = sb("rstd2", [P, GT])
        score = sb("score", [P, GT, E])
        top = sb("top", [P, 2, GT])
        first_of = sb("first_of", [P, 2, GT])
        tied = sb("tied", [P, GT, E])
        rest = sb("rest", [P, GT, E])
        onehot = sb("onehot", [P, 2, GT, E])
        both = sb("both", [P, GT + 1, E], BF16)
        base = sb("base", [P, E])
        base0 = sb("base0", [P, E])
        place = sb("place", [P, GT, E])
        picked = sb("picked", [P, 2, GT, E])
        dest = [sb(f"dest{i}", [P, 2, GT], I32) for i in range(2)]
        step_k = sb("step_k", [1, E, MAXT])
        t_cnt = sb("t_cnt", [1, E])
        t_gt = sb("t_gt", [1, E, MAXT])
        t_nt = sb("t_nt", [1, E])
        upto = sb("upto", [1, E, E])
        t_m = sb("t_m", [1, E, E])
        t_end = sb("t_end", [1, E])
        t_idx = sb("t_idx", [1, NTILE, E])
        t_ge = sb("t_ge", [1, NTILE, E])
        t_gn = sb("t_gn", [1, NTILE, E])
        t_e = sb("t_e", [1, NTILE])
        t_s = sb("t_s", [1, NTILE])
        t_o = sb("t_o", [1, NTILE])
        table = sb("table", [1, 2, NTILE], I32)
        tail = sb("tail", [1, E], I32)
        slot = [sb(f"slot{i}", [P, J, ROW]) for i in range(4)]
        xeT = [sb(f"xeT{i}", [P, TILE]) for i in range(2)]
        hT = [sb(f"hT{i}", [P, HC, TILE]) for i in range(2)]
        ye = [sb(f"ye{i}", [P, J, D]) for i in range(4)]
        share = [sb(f"share{i}", [P, J]) for i in range(4)]
        share_e = [sb(f"share_e{i}", [P, J]) for i in range(4)]
        share_n = [sb(f"share_n{i}", [P, J]) for i in range(4)]
        share_d = [sb(f"share_d{i}", [P, J]) for i in range(4)]
        yb = [sb(f"yb{i}", [P, J, D]) for i in range(2)]
        goes = [sb(f"goes{i}", [P, J], I32) for i in range(4)]
        F1raw = adj_in[0][:, :, :].rearrange("p a n -> p (a n)").rearrange("p (c d) -> p c d", d=D)
        F2raw = adj_in[1][:, :, :].rearrange("p a n -> p (a n)").rearrange("p (e h) -> p e h", h=H)
        flat = [a[:, :, :].rearrange("p a n -> p (a n)") for a in adj_in]
        wcur = [flat[i // 2][:, (i % 2) * WROW:(i % 2 + 1) * WROW] for i in range(4)]

        def bank(name):
            return ctx.enter_context(nc.psum_tensor(name, [P, 512], FP32))
        ps_t = [bank(f"ps_t{i}") for i in range(2)]
        ps_agg = bank("ps_agg")
        ps_h = [bank(f"ps_h{i}") for i in range(2)]
        ps_y = bank("ps_y")
        ps_x = bank("ps_x")
        ps_g = bank("ps_g")

        s_x0 = sem("x0_in")
        s_xr = sem("x_rest_in")
        s_adj = [sem(f"adj_in_sem{i}") for i in range(2)]
        s_const = sem("const_in")
        s_eps = sem("eps_in")
        s_F1 = sem("F1_in")
        s_F2 = sem("F2_in")
        s_fb2 = sem("fb2_in")
        s_ident = sem("ident_ready")
        s_made = sem("constants_made")
        s_smallT = sem("small_transposed")
        s_smallc = sem("small_copied")
        s_epsid = sem("eps_ident_ready")
        s_epsadd = sem("eps_added")
        s_tp = sem("adj_transposed")
        s_evA = sem("adjT_even_ready")
        s_evD = sem("adjT_odd_ready")
        s_mm = sem("adj_product_done")
        s_xn = sem("xn_ready")
        s_agg = sem("aggT_ready")
        s_h = sem("h_done")
        s_hb = sem("hb_ready")
        s_ss = sem("squares_summed")
        s_rms = sem("rms_rstd_ready")
        s_hn = sem("hn_ready")
        s_hT = sem("hn_transposed")
        s_silu = sem("silu_ready")
        s_y = sem("y_done")
        s_x1 = sem("x1_ready")
        s_xb = sem("x_plus_b2_ready")
        s_mv1 = sem("ln1_stats_ready")
        s_rs1 = sem("ln1_rstd_ready")
        s_mv2 = sem("ln2_stats_ready")
        s_rs2 = sem("ln2_rstd_ready")
        s_row1 = sem("rows_first_ready")
        s_row2 = sem("rows_second_ready")
        s_xT = sem("xn2_transposed")
        s_xTc = sem("xn2T_ready")
        s_gate = sem("gate_done")
        s_both = sem("choices_ready")
        s_rank = sem("ranks_done")
        s_base = sem("base_updated")
        s_dest = sem("dest_ready")
        s_scat = [sem(f"rows_scattered{i}") for i in range(2)]
        s_dve = sem("dve_order")
        s_act = sem("act_order")
        s_pool = sem("pool_order")
        s_turn = sem("pool_turns")
        s_dve2 = sem("dve_share_order")
        s_turn_dve = sem("dve_turns")
        s_spare = sem("spare_rows_filled")
        s_tails = sem("tails_filled")
        s_table = sem("table_ready")
        s_wT = sem("weights_transposed")
        s_wTa = sem("weights_copied_act")
        s_wTd = sem("weights_copied_dve")
        s_fb1c = sem("fb1_copied")
        s_slot = [sem(f"slot_in{i}") for i in range(4)]
        s_wcur = [sem(f"wcur_in{i}") for i in range(4)]
        s_eT = sem("tile_transposed")
        s_eTc = sem("xeT_ready")
        s_goes = sem("goes_ready")
        s_l1 = sem("layer1_done")
        s_reluA = sem("relu_even_ready")
        s_reluD = sem("relu_odd_ready")
        s_l2 = sem("layer2_done")
        s_ye = sem("ye_ready")
        s_ysc = [sem(f"results_scattered{i}") for i in range(4)]
        s_exp = sem("share_exp_ready")
        s_share = sem("share_ready")
        s_yb = sem("biased_result_ready")
        s_stored = sem("x1_stored")

        adj_g = adj.rearrange("b (h t p) m -> (b h) p t m", h=GPB, p=P)
        x_t = x.rearrange("b (t p) d -> p (b t) d", p=P)
        out_t = out[0:TOK, :].rearrange("(t p) d -> p t d", p=P)

        def wait(eng, s, v):
            if not (isinstance(v, int) and v <= 0):
                eng.wait_ge(s, v)

        class Order:

            def __init__(self, eng, s, links):
                self.eng, self.s, self.links, self.base, self.k = eng, s, links, 0, 0

            def step(self, base):
                self.base, self.k = base, 0

            def link(self, ins):
                self.k += 1
                ins.then_inc(self.s, 1)
                self.eng.wait_ge(self.s, self.base + self.k)

            def end(self):
                assert self.k <= self.links, self.k
                if self.k < self.links:
                    self.eng.sem_inc(self.s, self.links - self.k)

        def first_part(eng, step, last):
            def peeled(g):
                step(g, g % 2, g // 2)
            for g in range(4):
                peeled(g)
            with eng.Fori(2, B - 1) as b:
                for par in range(2):
                    step(b * 2 + par, par, b)
            for g in range(NG - 2, last + 1):
                peeled(g)

        def has(g, lag):
            return not isinstance(g, int) or 0 <= g - lag < NG

        LOOPED = (NTILE - 4) // 4

        def second_part(eng, step, lag):
            for t in range(4):
                step(t, t)
            with eng.Fori(1, 1 + LOOPED) as i:
                for k in range(4):
                    step(i * 4 + k, k)
            for t in range(4 + 4 * LOOPED, NTILE + lag):
                step(t, t % 4)

        def live(t, lag):
            return not isinstance(t, int) or 0 <= t - lag < NTILE

        def turn(t, k, n):
            return (t - k % n) // n if isinstance(t, int) else None

        block = ctx.enter_context(nc.Block())

        def fill_tails(eng, experts):
            for e in experts:
                row = eng.value_load(tail[0:1, e:e + 1], min_val=e * R, max_val=e * R + TOK)
                eng.dma_start(slots[bass.ds(row, TILE), :].rearrange("(p j) c -> p j c", j=J),
                              pad_rows[:, :, :]).then_inc(s_tails, 16)

        @block.sync
        def _(sp):
            sp.dma_start(epss[:, :], eps.to_broadcast([P, 1])).then_inc(s_eps, 16)
            sp.dma_start(x_all[:, 0:TPB, :], x_t[:, 0:TPB, :]).then_inc(s_x0, 16)
            sp.dma_start(adj_in[0][:, :, :], adj_g[0]).then_inc(s_adj[0], 16)
            sp.dma_start(adj_in[1][:, :, :], adj_g[1]).then_inc(s_adj[1], 16)
            sp.wait_ge(s_const, 16 * 9)
            sp.dma_start(x_all[:, TPB:NT, :], x_t[:, TPB:NT, :]).then_inc(s_xr, 16)
            def load_group(b):
                for par in range(2):
                    g = b * 2 + par
                    sp.wait_ge(s_tp, b * (2 * TPB) + (par - 1) * TPB)
                    src = adj_g[g] if isinstance(g, int) else adj_g[bass.ds(g, 1)].rearrange("o p t m -> (o p) t m")
                    sp.dma_start(adj_in[par][:, :, :], src).then_inc(s_adj[par], 16)
                    if has(g, 4):
                        store_x1(g - 4)

            def store_x1(q):
                sp.wait_ge(s_x1, q + 1)
                a, z = q * GT, (q + 1) * GT
                dst, src = ((out_t[:, a:z, :], x_all[:, a:z, :]) if isinstance(q, int) else
                            (out_t[:, bass.ds(a, GT), :], x_all[:, bass.ds(a, GT), :]))
                sp.dma_start(dst, src).then_inc(s_stored, 16)
            load_group(1)
            with sp.Fori(2, B) as b:
                load_group(b)
            sp.wait_ge(s_tp, TPB * (NG - 1))
            sp.dma_start(F1raw, F1.rearrange("e (c p) d -> p (e c) d", p=P)).then_inc(s_F1, 16)
            sp.wait_ge(s_tp, TPB * NG)
            sp.dma_start(F2raw, F2.rearrange("e d h -> d e h")).then_inc(s_F2, 16)
            for q in range(NG - 4, NG):
                store_x1(q)

            sp.wait_ge(s_table, 1)
            fill_tails(sp, range(0, E // 2))
            sp.wait_ge(s_tails, 16 * E)
            sp.wait_ge(s_spare, 16 * (SPARE + 1))
            sp.wait_ge(s_scat[0], 16 * GT * NG)
            sp.wait_ge(s_scat[1], 16 * GT * NG)
            sp.wait_ge(s_wTa, 2 * E)
            sp.wait_ge(s_fb1c, 1)
            sp.wait_ge(s_fb2, 16)

            def load(t, k):
                expert = sp.value_load(table[0:1, 0, bass.ds(t, 1)], min_val=0, max_val=E - 1)
                first = sp.value_load(table[0:1, 1, bass.ds(t, 1)], min_val=0,
                                      max_val=E * R + (SPARE - 1) * TILE)
                wait(sp, s_eT, t - 3)
                wait(sp, s_goes, t - 3)
                wait(sp, s_share, t - 3)
                sp.dma_start(slot[k][:, :, :], slots[bass.ds(first, TILE), :]
                             .rearrange("(p j) c -> p j c", j=J)).then_inc(s_slot[k], 16)
                wait(sp, s_l2, t - 3)
                wait(sp, s_yb, t - 3)
                sp.dma_start(wcur[k],
                             weights[:, bass.ds(expert, 1), :].rearrange("p o w -> p (o w)")
                             ).then_inc(s_wcur[k], 16)
            second_part(sp, load, 0)


        @block.tensor
        def _(pe):
            pe.wait_ge(s_ident, 1)

            def expert_weights(n):
                e = n // 2
                wait(pe, s_wTa, n - 1)
                for c in range(HC):
                    src = F2raw[:, e, c * P:(c + 1) * P] if n % 2 else F1raw[:, e * HC + c, :]
                    ins = pe.transpose(ps_t[n % 2][:, c * P:(c + 1) * P], src, ident[:, :])
                ins.then_inc(s_wT, 1)

            def step(g, par, b):
                def T(m):
                    if m == 0:
                        pe.wait_ge(s_epsadd, 4 * g + 4)
                    wait(pe, s_evD if m % 2 else s_evA, 4 * g + m // 2)
                    for j in range(GT):
                        ins = pe.transpose(ps_t[m % 2][:, j * P:(j + 1) * P],
                                           adj_in[par][:, j, m * P:(m + 1) * P], ident[:, :])
                    ins.then_inc(s_tp, 1)

                def M(m):
                    if m == 0:
                        if par == 0:
                            pe.wait_ge(s_xn, b + 1)
                        wait(pe, s_agg, g)
                    pe.wait_ge(s_evD if m % 2 else s_evA, 4 * g + m // 2 + 1)
                    pe.matmul(ps_agg[:, :], xn[:, m, :], adjT[:, m % 4, :],
                              start=(m == 0), stop=(m == TPB - 1)).then_inc(s_mm, 1)

                def tm(m):
                    if has(g, 0):
                        T(m)
                        if m >= 1:
                            M(m - 1)

                tm(0)
                tm(1)
                tm(2)
                if has(g, 1):
                    q = g - 1
                    pe.wait_ge(s_agg, q + 1)
                    for j in range(GT):
                        if j < 2:
                            wait(pe, s_silu, 4 * q - 1 + j)
                        else:
                            pe.wait_ge(s_hb, 4 * q + j - 1)
                        pe.matmul(ps_h[j % 2][:, :], aggT[1 - par][:, j * P:(j + 1) * P], W1s[:, :],
                                  start=True, stop=True).then_inc(s_h, 1)
                tm(3)
                if has(g, 2):
                    q = g - 2
                    pe.wait_ge(s_row1, q + 1)
                    for j in range(GT):
                        ins = pe.transpose(ps_x[:, j * P:(j + 1) * P], rows[par][:, 0, j, 0:D], ident[:, :])
                    ins.then_inc(s_xT, 1)
                if isinstance(g, int) and g == NG + 1:
                    for n in range(E, 2 * E):
                        expert_weights(n)
                tm(4)
                if has(g, 2):
                    q = g - 2
                    pe.wait_ge(s_xTc, q + 1)
                    if isinstance(q, int) and q == 0:
                        pe.wait_ge(s_smallc, 1)
                    wait(pe, s_base, q)
                    for j in range(GT):
                        ins = pe.matmul(ps_g[:, j * E:(j + 1) * E], xn2T[:, j * P:(j + 1) * P], WgT,
                                        start=True, stop=True)
                    ins.then_inc(s_gate, 1)
                tm(5)
                if has(g, 1):
                    q = g - 1
                    pe.wait_ge(s_hn, q + 1)
                    for c in range(HC):
                        if c >= 2:
                            pe.wait_ge(s_silu, 4 * q + c - 1)
                        for j in range(GT):
                            ins = pe.transpose(ps_h[c % 2][:, j * P:(j + 1) * P],
                                               hn[:, j, c * P:(c + 1) * P], ident[:, :])
                        ins.then_inc(s_hT, 1)
                tm(6)
                if has(g, 2):
                    q = g - 2
                    pe.wait_ge(s_both, q + 1)
                    pe.matmul(ps_g[:, 0:(GT + 1) * E], earlier[:, :],
                              both[:, :, :].rearrange("p t e -> p (t e)"), start=True, stop=False)
                    for j in range(GT):
                        n = GT - j
                        ins = pe.matmul(ps_g[:, (j + 1) * E:(GT + 1) * E].rearrange("p (n e) -> p n e", e=E),
                                        ones[:, :], both[:, j:j + 1, :].broadcast_to([P, n, E]),
                                        start=False, stop=(j == GT - 1))
                    ins.then_inc(s_rank, 1)
                tm(7)
                if has(g, 1):
                    q = g - 1
                    pe.wait_ge(s_silu, 4 * q + 4)
                    wait(pe, s_x1, q)
                    for j in range(GT):
                        for c in range(HC):
                            ins = pe.matmul(ps_y[:, j * P:(j + 1) * P], siluT[:, c, j * P:(j + 1) * P],
                                            W2s[:, c, :], start=(c == 0), stop=(c == HC - 1))
                    ins.then_inc(s_y, 1)
                if isinstance(g, int) and g == NG:
                    pe.wait_ge(s_F1, 16)
                    pe.wait_ge(s_F2, 16)
                    pe.wait_ge(s_evA, 4 * NG)
                    pe.wait_ge(s_evD, 4 * NG)
                    for n in range(E):
                        expert_weights(n)
                if has(g, 0):
                    M(TPB - 1)
                if isinstance(g, int) and g == 0:
                    pe.wait_ge(s_const, 16 * 9)
                    pe.transpose(ps_g[:, 0:NS], small[:, :], ident[0:NS, 0:NS]).then_inc(s_smallT, 1)
            first_part(pe, step, NG + 1)

            ps_e = [ps_t[0], ps_t[1]]
            ps_1 = [ps_agg, ps_h[0], ps_h[1], ps_x]
            ps_2 = [ps_y, ps_g]

            def tile(t, k):
                if live(t, 0):
                    pe.wait_ge(s_slot[k], 16 * (t // 4 + 1) if isinstance(t, int) else t * 4 + (16 - 4 * k))
                    wait(pe, s_eTc, t - 1)
                    for j in range(J):
                        ins = pe.transpose(ps_e[k % 2][:, j * P:(j + 1) * P], slot[k][:, j, 0:D], ident[:, :])
                    ins.then_inc(s_eT, 1)
                if live(t, 1):
                    u, ku = t - 1, (k - 1) % 4
                    pe.wait_ge(s_eTc, u + 1)
                    pe.wait_ge(s_wcur[ku],
                               16 * (u // 4 + 1) if isinstance(u, int) else u * 4 + (16 - 4 * ku))
                    for c in range(HC):
                        wait(pe, s_reluD if c % 2 else s_reluA, 2 * (u - 1) + c // 2 + 1)
                        pe.matmul(ps_1[c][:, 0:TILE], wcur[ku][:, CW1 + c * P:CW1 + (c + 1) * P],
                                  xeT[ku % 2][:, :], start=True, stop=True).then_inc(s_l1, 1)
                if live(t, 2):
                    u, ku = t - 2, (k - 2) % 4
                    pe.wait_ge(s_reluA, 2 * u + 2)
                    pe.wait_ge(s_reluD, 2 * u + 2)
                    wait(pe, s_yb, u - 1)
                    for j in range(J):
                        for c in range(HC):
                            ins = pe.matmul(ps_2[ku % 2][:, j * P:(j + 1) * P], hT[ku % 2][:, c, j * P:(j + 1) * P],
                                            wcur[ku][:, CW2 + c * D:CW2 + (c + 1) * D],
                                            start=(c == 0), stop=(c == HC - 1))
                    ins.then_inc(s_l2, 1)
            second_part(pe, tile, 2)

        @block.scalar
        def _(act):
            act.wait_ge(s_adj[0], 16)
            act.dma_start(small[0:HC, :], rms_w.rearrange("(c p) -> c p", p=P)).then_inc(s_const, 16)
            act.dma_start(small[HC:HC + E * HC, :], fb1.rearrange("e (c p) -> (e c) p", p=P)).then_inc(s_const, 16)
            act.dma_start(small[HC + E * HC:NS, :], Wg[:, :]).then_inc(s_const, 16)
            act.dma_start(W1s[:, :], W1[:, :]).then_inc(s_const, 16)
            act.dma_start(b1s[:, :], b1[None, :].to_broadcast([P, H])).then_inc(s_const, 16)
            act.dma_start(b2s[:, :], b2[None, :].to_broadcast([P, D])).then_inc(s_const, 16)
            act.dma_start(bgs[:, :], bg[None, :].to_broadcast([P, E])).then_inc(s_const, 16)
            act.dma_start(W2s[:, 0:2, :], W2[0:H // 2, :].rearrange("(c p) d -> p c d", p=P)).then_inc(s_const, 16)
            act.dma_start(W2s[:, 2:4, :], W2[H // 2:H, :].rearrange("(c p) d -> p c d", p=P)).then_inc(s_const, 16)
            act.dma_start(weights[:, :, CB2:CB2 + D], fb2[None, :, :].to_broadcast([P, E, D])).then_inc(s_fb2, 16)

            def copy_weights(n):
                act.wait_ge(s_wT, n + 1)
                at = CW2 if n % 2 else CW1
                act.activation(weights[:, n // 2, at:at + H], ps_t[n % 2][:, :], ACT.Copy).then_inc(s_wTa, 1)

            def step(g, par, b):
                def evac(m):
                    if has(g, 0):
                        act.wait_ge(s_tp, TPB * g + m + 1)
                        wait(act, s_mm, TPB * g + m - 3)
                        act.activation(adjT[:, m % 4, :], ps_t[m % 2][:, :], ACT.Copy).then_inc(s_evA, 1)
                evac(0)
                evac(2)
                if has(g, 1):
                    q = g - 1
                    wait(act, s_rms, q)
                    wait(act, s_hT, 4 * q)
                    for j in range(GT):
                        act.wait_ge(s_hb, 4 * q + j + 1)
                        act.activation(hn[:, j, :], hb[:, j, :], ACT.Square,
                                       accum_out=ss[:, j:j + 1]).then_inc(s_ss, 1)
                if has(g, 2):
                    q = g - 2
                    act.wait_ge(s_xT, q + 1)
                    wait(act, s_gate, q)
                    act.activation(xn2T[:, :], ps_x[:, :], ACT.Copy).then_inc(s_xTc, 1)
                    act.wait_ge(s_row1, q + 1)
                    act.activation(rows[par][:, 1, :, 0:D], rows[par][:, 0, :, 0:D], ACT.Copy).then_inc(s_row2, 1)
                if isinstance(g, int) and g == NG + 1:
                    for n in range(E, 2 * E):
                        copy_weights(n)
                evac(4)
                if isinstance(g, int) and g == 1:
                    act.wait_ge(s_smallc, 1)
                    act.activation(weights[:, :, CB1:CB1 + HC], fb1T.rearrange("p (e c) -> p e c", c=HC),
                                   ACT.Copy).then_inc(s_fb1c, 1)
                if has(g, 1):
                    q = g - 1
                    wait(act, s_y, q)
                    for c in range(HC):
                        act.wait_ge(s_hT, 4 * q + c + 1)
                        act.activation(siluT[:, c, :], ps_h[c % 2][:, :], ACT.Silu,
                                       scale=rmsT[:, c:c + 1]).then_inc(s_silu, 1)
                if isinstance(g, int) and g == NG:
                    for n in range(E):
                        copy_weights(n)
                evac(6)
            first_part(act, step, NG + 1)

            act.wait_ge(s_table, 1)
            fill_tails(act, range(E // 2, E))

            ps_1 = [ps_agg, ps_h[0], ps_h[1], ps_x]

            def tile(t, k):
                if live(t, 0):
                    act.wait_ge(s_slot[k], 16 * (t // 4 + 1) if isinstance(t, int) else t * 4 + (16 - 4 * k))
                    wait(act, s_share, t - 3)
                    act.activation(share_e[k][:, :], slot[k][:, :, GAP], ACT.Exp).then_inc(s_exp, 1)
                if live(t, 1):
                    u, ku = t - 1, (k - 1) % 4
                    for c in (0, 2):
                        act.wait_ge(s_l1, 4 * u + c + 1)
                        wait(act, s_l2, u - 1)
                        act.activation(hT[ku % 2][:, c, :], ps_1[c][:, 0:TILE], ACT.Relu,
                                       bias=wcur[ku][:, CB1 + c:CB1 + c + 1]).then_inc(s_reluA, 1)
                if live(t, 2):
                    u, ku = t - 2, (k - 2) % 4
                    act.wait_ge(s_share, u + 1)
                    act.wait_ge(s_yb, u + 1)
                    wait(act, s_ysc[ku], (u // 4) * 16 * J if isinstance(u, int) else (u - ku) * (4 * J))
                    for j in range(J):
                        ins = act.activation(ye[ku][:, j, :], yb[ku % 2][:, j, :], ACT.Copy, scale=share[ku][:, j:j + 1])
                    ins.then_inc(s_ye, 1)
            second_part(act, tile, 2)

        @block.gpsimd
        def _(pool):
            order = Order(pool, s_pool, 4)
            order.step(0)
            pool.memset(ident[:, :], 0.0)
            pool.memset(minus_half[:, :], -0.5)
            pool.memset(ln_eps[:, :], 1e-5)
            pool.memset(rms_eps[:, :], 1e-6 * H)
            pool.memset(earlier[:, :], 1.0)
            pool.memset(pad_rows[:, :, :], 0.0)
            order.link(pool.memset(ones[:, :], 1.0))
            pool.affine_select(out=ident[:, :], in_=ident[:, :], compare_op=ALU.not_equal, fill=1.0, base=0,
                               pattern=[[-1, P]], channel_multiplier=1).then_inc(s_ident, 1)
            pool.affine_select(out=earlier[:, :], in_=earlier[:, :], compare_op=ALU.is_gt, fill=0.0, base=0,
                               pattern=[[1, P]], channel_multiplier=-1)
            pool.iota(token_id[:, :], [[P, NT]], base=0, channel_multiplier=1,
                      allow_small_or_imprecise_dtypes=True)
            for i in range(2):
                for c in range(2):
                    pool.memset(rows[i][:, c, :, CHOICE:CHOICE + 1], float(c))
            pool.iota(falling[:, :, :], [[0, GT], [-1, E]], base=E, channel_multiplier=0,
                      allow_small_or_imprecise_dtypes=True)
            pool.iota(base0[:, :], [[R, E]], base=0, channel_multiplier=0, allow_small_or_imprecise_dtypes=True)
            pool.iota(step_k[:, :, :], [[0, E], [TILE, MAXT]], base=0, channel_multiplier=0,
                      allow_small_or_imprecise_dtypes=True)
            pool.iota(t_idx[:, :, :], [[1, NTILE], [0, E]], base=0, channel_multiplier=0,
                      allow_small_or_imprecise_dtypes=True)
            pool.iota(upto[:, :, :], [[1, E], [-1, E]], base=0, channel_multiplier=0,
                      allow_small_or_imprecise_dtypes=True)
            order.link(pool.iota(pad_rows[:, :, ID], [[1, J]], base=TOK, channel_multiplier=J,
                                 allow_small_or_imprecise_dtypes=True))
            pool.memset(both_pad := both[:, GT:GT + 1, :], 0.0).then_inc(s_made, 1)
            pool.wait_ge(s_eps, 16)
            order.link(pool.tensor_scalar(eps_ident[:, :], ident[:, :], epss[:, 0:1], 1.0, ALU.mult, ALU.mult))
            def inv_sqrt(square_, eps_, scratch, result, n, s_done):
                order.link(pool.tensor_tensor(scratch, square_, eps_[:, 0:n], ALU.add))
                pool.tensor_tensor(result, scratch, minus_half[:, 0:n], ALU.pow).then_inc(s_done, 1)

            def add_eps(g, par, b):
                pool.wait_ge(s_adj[par], 16 * b + 16)
                for j in range(GT):
                    col = (par * GT + j) * P
                    pool.tensor_tensor(adj_in[par][:, j, col:col + P], adj_in[par][:, j, col:col + P],
                                       eps_ident[:, :], ALU.add).then_inc(s_epsadd, 1)

            def x_plus_b2(b):
                xv = x_all[:, bass.ds(b * TPB, TPB), :] if not isinstance(b, int) else x_all[:, b * TPB:(b + 1) * TPB, :]
                pool.tensor_tensor(xv, xv, b2s[:, None, :].broadcast_to([P, TPB, D]), ALU.add).then_inc(s_xb, 1)

            pool.wait_ge(s_mv1, 1)
            inv_sqrt(mv1[:, :, 1], ln_eps, ve1[:, :], rstd1[:, :], TPB, s_rs1)
            add_eps(0, 0, 0)
            order.end()
            for n in range(SPARE):
                r = E * R + n * TILE
                pool.dma_start(slots[r:r + TILE, :].rearrange("(p j) c -> p j c", j=J),
                               pad_rows[:, :, :]).then_inc(s_spare, 16)
            pool.dma_start(out[TOK:TOK + TILE, :].rearrange("(p j) d -> p j d", j=J),
                           pad_rows[:, :, 0:D]).then_inc(s_spare, 16)

            def scatter_rows(g, par, c):
                for j in range(GT):
                    pool.indirect_dma_start(
                        out=slots, out_offset=bass.IndirectOffsetOnAxis(ap=dest[1 - par][:, c, j:j + 1], axis=0),
                        in_=rows[1 - par][:, c, j, :], in_offset=None,
                        bounds_check=E * R - 1, oob_is_err=True).then_inc(s_scat[1 - par], 16)

            def step(g, par, b):
                order.step((g + 1) * 4)
                if has(g, 3):
                    pool.wait_ge(s_dest, g - 2)
                    pool.wait_ge(s_row2, g - 2)
                if has(g, 1):
                    q = g - 1
                    pool.wait_ge(s_ss, 4 * q + 4)
                    wait(pool, s_hn, q)
                    inv_sqrt(ss[:, :], rms_eps, rms_var[:, :], rms_rstd[:, :], GT, s_rms)
                if has(g, -1):
                    add_eps(g + 1, 1 - par, b + par)
                if isinstance(g, int) and g == 0:
                    pool.wait_ge(s_const, 16 * 9)
                if par == 0 and has(g, 0):
                    pool.wait_ge(s_xn, b + 1)
                    pool.sem_inc(s_turn, 1)
                    x_plus_b2(b)
                if has(g, 3):
                    for c in range(2):
                        if not (isinstance(g, int) and g == NG + 1 and c == 0):
                            scatter_rows(g, par, c)
                if isinstance(g, int) and g == NG:
                    pool.wait_ge(s_dest, g - 1)
                    pool.wait_ge(s_row2, g - 1)
                    scatter_rows(g + 1, 1 - par, 0)
                if par == 1 and has(g, -1):
                    pool.wait_ge(s_mv1, b + 2)
                    inv_sqrt(mv1[:, :, 1], ln_eps, ve1[:, :], rstd1[:, :], TPB, s_rs1)
                if has(g, 1):
                    q = g - 1
                    pool.wait_ge(s_mv2, q + 1)
                    wait(pool, s_row1, q)
                    inv_sqrt(mv2[:, :, 1], ln_eps, ve2[:, :], rstd2[:, :], GT, s_rs2)
                order.end()
            first_part(pool, step, NG + 2)

            pool.wait_ge(s_stored, 16 * NG)
            pool.wait_ge(s_spare, 16 * (SPARE + 1))

            def add_results(t, k):
                if live(t, 2):
                    u, ku = t - 2, (k - 2) % 4
                    pool.wait_ge(s_ye, u + 1)
                    pool.wait_ge(s_goes, u + 1)
                    prev = u - 1
                    if not (isinstance(u, int) and u == 0):
                        pool.wait_ge(s_ysc[(ku - 1) % 4],
                                     (prev // 4 + 1) * 16 * J if isinstance(u, int)
                                     else prev * (4 * J) + (4 - (ku - 1) % 4) * (4 * J))
                    pool.sem_inc(s_turn, 1)
                    for j in range(J):
                        pool.indirect_dma_start(
                            out=out, out_offset=bass.IndirectOffsetOnAxis(ap=goes[ku][:, j:j + 1], axis=0),
                            in_=ye[ku][:, j, :], in_offset=None, bounds_check=TOK + TILE - 1,
                            compute_op=ALU.add).then_inc(s_ysc[ku], 16)
            second_part(pool, add_results, 2)
            for k in range(4):
                pool.wait_ge(s_ysc[k], 16 * J * ((NTILE + 3 - k) // 4))

        @block.vector
        def _(dve):
            order = Order(dve, s_dve, 21)
            order.step(0)

            def token_tile(t):
                return x_all[:, t, :] if isinstance(t, int) else x_all[:, bass.ds(t, 1), :].rearrange("p o d -> p (o d)")

            def ln1_stats(b):
                for j in range(TPB):
                    ins = dve.bn_stats(st1[:, j, :], token_tile(b * TPB + j))
                order.link(ins)
                wait(dve, s_rs1, b)

            def ln1_aggregate(b):
                for j in range(TPB):
                    ins = dve.bn_aggr(mv1[:, j, :], st1[:, j, :])
                ins.then_inc(s_mv1, 1)

            def ln1_norm(b):
                dve.wait_ge(s_rs1, b + 1)
                for j in range(TPB):
                    ins = dve.tensor_scalar(xn[:, j, :], token_tile(b * TPB + j), mv1[:, j, 0:1], rstd1[:, j:j + 1],
                                            ALU.subtract, ALU.mult)
                ins.then_inc(s_xn, 1)

            dve.wait_ge(s_x0, 16)
            ln1_stats(0)
            ln1_aggregate(0)
            dve.wait_ge(s_made, 1)
            dve.tensor_copy(base[:, :], base0[:, :])
            dve.tensor_scalar(upto[:, :, :], upto[:, :, :], 0.0, None, ALU.is_ge)
            ln1_norm(0)
            order.end()

            def step(g, par, b):
                order.step((g + 1) * 21)

                def evac(m):
                    if has(g, 0):
                        dve.wait_ge(s_tp, TPB * g + m + 1)
                        wait(dve, s_mm, TPB * g + m - 3)
                        dve.tensor_copy(adjT[:, m % 4, :], ps_t[m % 2][:, :]).then_inc(s_evD, 1)
                evac(1)
                if has(g, 2):
                    q = g - 2
                    wait(dve, s_scat[par], (q // 2) * 128 if isinstance(q, int) else (q - par) * 64)
                    ids = token_id[:, q * GT:(q + 1) * GT] if isinstance(q, int) else token_id[:, bass.ds(q * GT, GT)]
                    dve.tensor_copy(rows[par][:, :, :, ID], ids[:, None, :].broadcast_to([P, 2, GT]))
                    dve.wait_ge(s_rs2, q + 1)
                    for j in range(GT):
                        ins = dve.tensor_scalar(rows[par][:, 0, j, 0:D], token_tile(q * GT + j), mv2[:, j, 0:1],
                                                rstd2[:, j:j + 1], ALU.subtract, ALU.mult)
                    ins.then_inc(s_row1, 1)
                if has(g, 1):
                    q = g - 1
                    for j in range(GT):
                        dve.wait_ge(s_h, 4 * q + j + 1)
                        dve.tensor_tensor(hb[:, j, :], ps_h[j % 2][:, :], b1s[:, :], ALU.add).then_inc(s_hb, 1)
                evac(3)
                if has(g, 1):
                    q = g - 1
                    dve.wait_ge(s_rms, q + 1)
                    wait(dve, s_hT, 4 * q)
                    for j in range(GT):
                        ins = dve.tensor_scalar(hn[:, j, :], hb[:, j, :], rms_rstd[:, j:j + 1], float(H) ** 0.5,
                                                ALU.mult, ALU.mult)
                    ins.then_inc(s_hn, 1)
                evac(5)
                if has(g, 2):
                    q = g - 2
                    dve.wait_ge(s_gate, q + 1)
                    order.link(dve.tensor_tensor(score[:, :, :], ps_g[:, 0:GT * E].rearrange("p (t e) -> p t e", e=E),
                                                 bgs[:, None, :].broadcast_to([P, GT, E]), ALU.add))
                    src = score
                    for c in range(2):
                        order.link(dve.reduce_max(top[:, c, :], src[:, :, :], AX.X))
                        order.link(dve.tensor_tensor(tied[:, :, :], src[:, :, :],
                                                     top[:, c, :, None].broadcast_to([P, GT, E]), ALU.is_equal))
                        order.link(dve.tensor_tensor(tied[:, :, :], tied[:, :, :], falling[:, :, :], ALU.mult))
                        order.link(dve.reduce_max(first_of[:, c, :], tied[:, :, :], AX.X))
                        order.link(dve.tensor_tensor(onehot[:, c, :, :], falling[:, :, :],
                                                     first_of[:, c, :, None].broadcast_to([P, GT, E]), ALU.is_equal))
                        if c == 0:
                            order.link(dve.scalar_tensor_tensor(rest[:, :, :], onehot[:, 0, :, :], -BIG, score[:, :, :],
                                                                ALU.mult, ALU.add))
                            src = rest
                    dve.tensor_tensor(both[:, 0:GT, :], onehot[:, 0, :, :], onehot[:, 1, :, :], ALU.add).then_inc(s_both, 1)
                    order.link(dve.tensor_tensor(rows[par][:, :, :, GAP], top[:, 1, None, :].broadcast_to([P, 2, GT]),
                                                 top[:, 0, None, :].broadcast_to([P, 2, GT]), ALU.subtract))
                if par == 1 and has(g, -1):
                    if isinstance(b, int) and b == 0:
                        dve.wait_ge(s_xr, 16)
                    ln1_stats(b + 1)
                evac(7)
                if par == 1 and has(g, -1):
                    ln1_aggregate(b + 1)
                if has(g, 2):
                    q = g - 2
                    dve.wait_ge(s_rank, q + 1)
                    order.link(dve.tensor_tensor(place[:, :, :], ps_g[:, 0:GT * E].rearrange("p (t e) -> p t e", e=E),
                                                 base[:, None, :].broadcast_to([P, GT, E]), ALU.add))
                    dve.tensor_tensor(base[:, :], base[:, :], ps_g[:, GT * E:(GT + 1) * E], ALU.add).then_inc(s_base, 1)
                    order.link(dve.tensor_tensor(picked[:, :, :, :], onehot[:, :, :, :],
                                                 place[:, None, :, :].broadcast_to([P, 2, GT, E]), ALU.mult))
                    wait(dve, s_scat[par], (q // 2) * 128 if isinstance(q, int) else (q - par) * 64)
                    with nc.allow_low_precision(reason="sums of whole numbers below 2**24, one of them not zero"):
                        dve.tensor_reduce(dest[par][:, :, :].rearrange("p c t -> p (c t)"),
                                          picked[:, :, :, :].rearrange("p c t e -> p (c t) e"),
                                          AX.X, ALU.add).then_inc(s_dest, 1)
                if has(g, 1):
                    q = g - 1
                    dve.wait_ge(s_y, q + 1)
                    dve.wait_ge(s_xb, b + par)
                    xv = x_all[:, q * GT:(q + 1) * GT, :] if isinstance(q, int) else x_all[:, bass.ds(q * GT, GT), :]
                    ins = dve.tensor_tensor(xv, ps_y[:, :].rearrange("p (t d) -> p t d", d=D), xv, ALU.add)
                    order.k += 1
                    ins.then_inc(s_x1, 1)
                    order.k -= 1
                if has(g, 1):
                    dve.wait_ge(s_x1, g)
                if has(g, 0):
                    dve.wait_ge(s_mm, TPB * g + TPB)
                    wait(dve, s_h, 4 * (g - 1))
                    dve.tensor_copy(aggT[par][:, :], ps_agg[:, :]).then_inc(s_agg, 1)
                if par == 1 and has(g, -1):
                    ln1_norm(b + 1)
                if isinstance(g, int) and g == 0:
                    dve.wait_ge(s_smallT, 1)
                    dve.tensor_copy(smallT[:, :], ps_g[:, 0:NS]).then_inc(s_smallc, 1)
                if has(g, 1):
                    q = g - 1
                    for j in range(GT):
                        ins = dve.bn_stats(st2[:, j, :], token_tile(q * GT + j))
                    order.link(ins)
                    dve.sem_inc(s_turn_dve, 1)
                    for j in range(GT):
                        ins = dve.bn_aggr(mv2[:, j, :], st2[:, j, :])
                    ins.then_inc(s_mv2, 1)
                order.end()
            first_part(dve, step, NG + 1)

            order.step((NG + 3) * 21)
            dve.wait_ge(s_base, NG)
            dve.tensor_copy(tail[:, :], base[0:1, :])
            order.link(dve.tensor_tensor(t_cnt[:, :], base[0:1, :], base0[0:1, :], ALU.subtract))
            order.link(dve.tensor_tensor(t_gt[:, :, :], t_cnt[:, :, None].broadcast_to([1, E, MAXT]), step_k[:, :, :], ALU.is_gt))
            order.link(dve.tensor_reduce(t_nt[:, :], t_gt[:, :, :], AX.X, ALU.add))
            order.link(dve.tensor_tensor(t_m[:, :, :], t_nt[:, None, :].broadcast_to([1, E, E]), upto[:, :, :], ALU.mult))
            order.link(dve.tensor_reduce(t_end[:, :], t_m[:, :, :], AX.X, ALU.add))
            order.link(dve.tensor_tensor(t_ge[:, :, :], t_idx[:, :, :], t_end[:, None, :].broadcast_to([1, NTILE, E]), ALU.is_ge))
            order.link(dve.tensor_tensor(t_gn[:, :, :], t_ge[:, :, :], t_nt[:, None, :].broadcast_to([1, NTILE, E]), ALU.mult))
            dve.tensor_reduce(t_e[:, :], t_ge[:, :, :], AX.X, ALU.add)
            order.link(dve.tensor_reduce(t_s[:, :], t_gn[:, :, :], AX.X, ALU.add))
            order.link(dve.tensor_tensor(t_o[:, :], t_idx[:, :, 0], t_s[:, :], ALU.subtract))
            order.link(dve.tensor_scalar(t_o[:, :], t_o[:, :], float(TILE), None, ALU.mult))
            dve.scalar_tensor_tensor(table[:, 1, :], t_e[:, :], float(R), t_o[:, :], ALU.mult, ALU.add)
            dve.tensor_scalar(table[:, 0, :], t_e[:, :], float(E - 1), None, ALU.min).then_inc(s_table, 1)
            order.end()

            ps_e = [ps_t[0], ps_t[1]]
            ps_1 = [ps_agg, ps_h[0], ps_h[1], ps_x]
            ps_2 = [ps_y, ps_g]

            shares = Order(dve, s_dve2, 2)

            def tile(t, k):
                if live(t, 0):
                    dve.wait_ge(s_eT, t + 1)
                    wait(dve, s_ysc[k], (t // 4) * 16 * J if isinstance(t, int) else (t - k) * (4 * J))
                    dve.tensor_copy(goes[k][:, :], slot[k][:, :, ID]).then_inc(s_goes, 1)
                    wait(dve, s_l1, 4 * (t - 1))
                    dve.tensor_copy(xeT[k % 2][:, :], ps_e[k % 2][:, 0:TILE]).then_inc(s_eTc, 1)
                    shares.step(t * 2)
                    dve.wait_ge(s_exp, t + 1)
                    dve.tensor_scalar(share_d[k][:, :], share_e[k][:, :], 1.0, None, ALU.add)
                    shares.link(dve.scalar_tensor_tensor(share_n[k][:, :], share_e[k][:, :], -1.0, slot[k][:, :, CHOICE],
                                                         ALU.add, ALU.mult))
                    shares.link(dve.reciprocal(share_d[k][:, :], share_d[k][:, :]))
                    wait(dve, s_ye, t - 3)
                    dve.scalar_tensor_tensor(share[k][:, :], share_n[k][:, :], 1.0, share_d[k][:, :],
                                             ALU.add, ALU.mult).then_inc(s_share, 1)
                if live(t, 1):
                    u, ku = t - 1, (k - 1) % 4
                    for c in (1, 3):
                        dve.wait_ge(s_l1, 4 * u + c + 1)
                        wait(dve, s_l2, u - 1)
                        dve.tensor_scalar(hT[ku % 2][:, c, :], ps_1[c][:, 0:TILE],
                                          wcur[ku][:, CB1 + c:CB1 + c + 1], 0.0,
                                          ALU.add, ALU.max).then_inc(s_reluD, 1)
                if live(t, 2):
                    u, ku = t - 2, (k - 2) % 4
                    dve.wait_ge(s_l2, u + 1)
                    wait(dve, s_ye, u - 1)
                    dve.tensor_tensor(yb[ku % 2][:, :, :], ps_2[ku % 2][:, 0:TILE].rearrange("p (j d) -> p j d", d=D),
                                      wcur[ku][:, None, CB2:CB2 + D].broadcast_to([P, J, D]), ALU.add).then_inc(s_yb, 1)
            second_part(dve, tile, 2)



_INS = ["x", "adj", "L0_gnn_epsilon", "L0_gnn_W1", "L0_gnn_b1", "L0_gnn_rms_weight", "L0_gnn_W2", "L0_gnn_b2",
        "L0_ffn_Wg", "L0_ffn_bg", "L0_ffn_W1", "L0_ffn_b1", "L0_ffn_W2", "L0_ffn_b2"]


def kernel(**inputs):
    import concourse.bacc as bacc
    from concourse.bass_utils import run_bass_kernel_spmd

    nc = bacc.Bacc("TRN2", target_bir_lowering=False, num_devices=1)
    arrays, args = {}, []
    for name in _INS:
        a = np.ascontiguousarray(inputs[name])
        if a.ndim == 0:
            a = a.reshape(1, 1)
        arrays[f"in_{name}"] = a
        args.append(nc.dram_tensor(f"in_{name}", a.shape, mybir.dt.from_np(a.dtype), kind="ExternalInput").ap())
    shape = inputs["x"].shape
    tokens = shape[0] * shape[1]
    args.append(nc.dram_tensor("out_0", (tokens + TILE, shape[2]), FP32, kind="ExternalOutput").ap())
    build(nc, *args)
    r = run_bass_kernel_spmd(nc, [arrays], core_ids=[0])
    return r.results[0]["out_0"][:tokens].reshape(shape)
```

```python
from contextlib import ExitStack

import numpy as np
import concourse.bass as bass
from concourse import mybir

FP32 = mybir.dt.float32
FP32R = mybir.dt.float32r
BF16 = mybir.dt.bfloat16
I32 = mybir.dt.int32
ALU = mybir.AluOpType
ACT = mybir.ActivationFunctionType
AX = mybir.AxisListType
P = 128
TILE = 384


def build(nc, x, adj, eps, W1, b1, rms_w, W2, b2, Wg, bg, F1, fb1, F2, fb2, out):
    B, N, D = x.shape
    H = W1.shape[1]
    E = Wg.shape[0]
    TOK = B * N
    NT = TOK // P
    TPB = N // P
    GT = 4
    GTOK = GT * P
    NG = NT // GT
    GPB = TPB // GT
    assert GPB == 2
    HC = H // P
    J = TILE // P
    NTILE = (2 * TOK + E * (TILE - 1)) // TILE
    MAXT = -(-TOK // TILE)
    R = TOK + TILE
    SPARE = NTILE - -(-2 * TOK // TILE)
    ID, GAP, CHOICE = D, D + 1, D + 2
    ROW = D + 3
    CB1, CB2 = 0, HC
    BROW = CB2 + D
    BIG = 3.0e38

    slots = nc.dram_tensor("slots", [E * R + SPARE * TILE, ROW], FP32, kind="Internal").ap()

    ctx = ExitStack()
    with ctx:
        def sb(name, shape, dt=FP32):
            return ctx.enter_context(nc.sbuf_tensor(name, shape, dt))

        def sem(name):
            return ctx.enter_context(nc.semaphore(name))

        x_all = sb("x_all", [P, NT, D])
        adj_in = [sb(f"adj_in{i}", [P, GT, N]) for i in range(2)]
        adjT_hi = [sb(f"adjT_hi{i}", [P, GTOK], FP32R) for i in range(2)]
        adjT_lo = [sb(f"adjT_lo{i}", [P, GTOK], FP32R) for i in range(2)]
        xn = sb("xn", [P, TPB, D])
        xn_hi = sb("xn_hi", [P, TPB, D], FP32R)
        xn_lo = sb("xn_lo", [P, TPB, D], FP32R)
        aggT_hi = sb("aggT_hi", [P, GTOK], FP32R)
        aggT_lo = sb("aggT_lo", [P, GTOK], FP32R)
        hb = sb("hb", [P, GT, H])
        hn = sb("hn", [P, GT, H])
        siluT = sb("siluT", [P, HC, GTOK])
        rows = [sb(f"rows{i}", [P, 2, GT, ROW]) for i in range(2)]
        xn2T = sb("xn2T", [P, GTOK])
        W1e = sb("W1e", [P, E, 2, H], FP32R)
        W1cur = [sb(f"W1cur{i}", [P, 2, H], FP32R) for i in range(2)]
        W1cur += [a[:, :, :].rearrange("p (s m) d -> p s (m d)", s=2) for a in (xn_hi, xn_lo)]
        W2e = sb("W2e", [P, E, H])
        biases = sb("biases", [P, E, BROW])
        W1_hi = sb("W1_hi", [P, H], FP32R)
        W1_lo = sb("W1_lo", [P, H], FP32R)
        W2s = sb("W2s", [P, HC, D])
        b1s = sb("b1s", [P, H])
        b2s = sb("b2s", [P, D])
        bgs = sb("bgs", [P, E])
        epss = sb("epss", [P, 1])
        NS = HC + E * HC + E
        small = sb("small", [NS, D])
        smallT = sb("smallT", [P, NS])
        rmsT, fb1T, WgT = smallT[:, 0:HC], smallT[:, HC:HC + E * HC], smallT[:, HC + E * HC:NS]
        ident = sb("ident", [P, P])
        eps_ident = sb("eps_ident", [P, P])
        earlier = sb("earlier", [P, P], BF16)
        ones = sb("ones", [P, P], BF16)
        minus_half = sb("minus_half", [P, TPB])
        ln_eps = sb("ln_eps", [P, TPB])
        zeros = sb("zeros", [P, TPB])
        rms_eps = sb("rms_eps", [P, TPB])
        falling = sb("falling", [P, GT, E])
        token_id = sb("token_id", [P, NT])
        pad_rows = sb("pad_rows", [P, J, ROW])
        ss = sb("ss", [P, GT])
        rms_var = sb("rms_var", [P, GT])
        rms_rstd = sb("rms_rstd", [P, GT])
        st1 = sb("st1", [P, TPB, 6])
        mv1 = sb("mv1", [P, TPB, 2])
        ve1 = sb("ve1", [P, TPB])
        rstd1 = sb("rstd1", [P, TPB])
        shift1 = sb("shift1", [P, TPB])
        st2 = sb("st2", [P, GT, 6])
        mv2 = sb("mv2", [P, GT, 2])
        ve2 = sb("ve2", [P, GT])
        rstd2 = sb("rstd2", [P, GT])
        score = sb("score", [P, GT, E])
        top = sb("top", [P, 2, GT])
        first_of = sb("first_of", [P, 2, GT])
        tied = sb("tied", [P, GT, E])
        rest = sb("rest", [P, GT, E])
        onehot = sb("onehot", [P, 2, GT, E])
        both = sb("both", [P, GT + 1, E], BF16)
        base = sb("base", [P, E])
        base0 = sb("base0", [P, E])
        place = sb("place", [P, GT, E])
        picked = sb("picked", [P, 2, GT, E])
        dest = [sb(f"dest{i}", [P, 2, GT], I32) for i in range(2)]
        step_k = sb("step_k", [1, E, MAXT])
        t_cnt = sb("t_cnt", [1, E])
        t_gt = sb("t_gt", [1, E, MAXT])
        t_nt = sb("t_nt", [1, E])
        upto = sb("upto", [1, E, E])
        t_m = sb("t_m", [1, E, E])
        t_end = sb("t_end", [1, E])
        t_idx = sb("t_idx", [1, NTILE, E])
        t_ge, t_gn = (hb[0:1, 2 * i:2 * i + 2, :].rearrange("o a h -> o (a h)")[:, 0:NTILE * E]
                      .rearrange("o (t e) -> o t e", e=E) for i in range(2))
        t_e = sb("t_e", [1, NTILE])
        t_s = sb("t_s", [1, NTILE])
        t_o = sb("t_o", [1, NTILE])
        t_new = sb("t_new", [1, NTILE])
        before = sb("before", [1, -(-NTILE // 4), 4])
        table = sb("table", [1, 2, NTILE], I32)
        t_wait = sb("t_wait", [1, NTILE - 1])
        earlier_adds = sb("earlier_adds", [1, NTILE - 1], I32)
        tail = sb("tail", [1, E], I32)
        share = [sb(f"share{i}", [P, J]) for i in range(4)]
        share_e = [sb(f"share_e{i}", [P, J]) for i in range(4)]
        share_n = [sb(f"share_n{i}", [P, J]) for i in range(4)]
        share_d = [sb(f"share_d{i}", [P, J]) for i in range(4)]
        goes = [sb(f"goes{i}", [P, J], I32) for i in range(4)]
        F1raw = adj_in[0][:, :, :].rearrange("p a n -> p (a n)").rearrange("p (c d) -> p c d", d=D)
        F2raw = adj_in[1][:, :, :].rearrange("p a n -> p (a n)").rearrange("p (e h) -> p e h", h=H)
        hT = [a[:, :, :].rearrange("p t h -> p (t h)")[:, 0:HC * TILE].rearrange("p (c t) -> p c t", c=HC)
              for a in (hb, hn)]
        xeT_hi = [a[:, 0:TILE] for a in adjT_hi]
        xeT_lo = [a[:, 0:TILE] for a in adjT_lo]
        pad_rows2 = hn[:, 0, 0:J * ROW].rearrange("p (j c) -> p j c", c=ROW)
        W1_raw = hb[:, 0, :]
        flat = [a[:, :, :].rearrange("p a n -> p (a n)") for a in adj_in]
        at = iter(range(0, flat[0].shape[1], J * D))
        block_of = [flat[0][:, o:o + J * D].rearrange("p (j d) -> p j d", d=D) for o in at if o + J * D <= flat[0].shape[1]]
        ye, yb = block_of[0:4], block_of[4:6]
        slot = [flat[1][:, 4 * BROW + i * J * ROW:4 * BROW + (i + 1) * J * ROW].rearrange("p (j c) -> p j c", c=ROW)
                for i in range(4)]
        bcur = [flat[1][:, i * BROW:(i + 1) * BROW] for i in range(4)]

        def bank(name):
            return ctx.enter_context(nc.psum_tensor(name, [P, 512], FP32))
        ps_t = [bank(f"ps_t{i}") for i in range(2)]
        ps_agg = [bank(f"ps_agg{i}") for i in range(2)]
        ps_h = [bank(f"ps_h{i}") for i in range(2)]
        ps_y = bank("ps_y")
        ps_g = bank("ps_g")

        s_x0 = sem("x0_in")
        s_xr = sem("x_rest_in")
        s_adj = [sem(f"adj_in_sem{i}") for i in range(2)]
        s_const = sem("const_in")
        s_eps = sem("eps_in")
        s_F1 = sem("F1_in")
        s_F2 = sem("F2_in")
        s_fb2 = sem("fb2_in")
        s_ident = sem("ident_ready")
        s_made = sem("constants_made")
        s_smallT = sem("small_transposed")
        s_smallc = sem("small_copied")
        s_epsid = sem("eps_ident_ready")
        s_epsadd = sem("eps_added")
        s_tp = sem("adj_transposed")
        s_hi = sem("adjT_hi_ready")
        s_lo = sem("adjT_lo_ready")
        s_xh = sem("xn_hi_ready")
        s_xl = sem("xn_lo_ready")
        s_aggh = sem("aggT_hi_ready")
        s_W1h = sem("W1_hi_ready")
        s_W1l = sem("W1_lo_ready")
        s_xs = sem("x_second_in")
        s_mm = sem("adj_product_done")
        s_xn = sem("xn_ready")
        s_agg = sem("aggT_ready")
        s_h = sem("h_done")
        s_hb = sem("hb_ready")
        s_ss = sem("squares_summed")
        s_rms = sem("rms_rstd_ready")
        s_hn = sem("hn_first_half_ready")
        s_hna = sem("hn_second_half_ready")
        s_hT = sem("hn_transposed")
        s_silu = sem("silu_ready")
        s_y = sem("y_done")
        s_x1 = sem("x1_ready")
        s_xb = sem("x_plus_b2_ready")
        s_mv1 = sem("ln1_stats_ready")
        s_rs1 = sem("ln1_rstd_ready")
        s_mv2 = sem("ln2_stats_ready")
        s_rs2 = sem("ln2_rstd_ready")
        s_row1 = sem("rows_first_ready")
        s_row2 = sem("rows_second_ready")
        s_xT = sem("xn2_transposed")
        s_xTc = sem("xn2T_ready")
        s_gate = sem("gate_done")
        s_both = sem("choices_ready")
        s_rank = sem("ranks_done")
        s_base = sem("base_updated")
        s_dest = sem("dest_ready")
        s_scat = [sem(f"rows_scattered{i}") for i in range(2)]
        s_dve = sem("dve_order")
        s_act = sem("act_order")
        s_pool = sem("pool_order")
        s_turn = sem("pool_turns")
        s_dve2 = sem("dve_share_order")
        s_turn_dve = sem("dve_turns")
        s_spare = sem("spare_rows_filled")
        s_tails = sem("tails_filled")
        s_tail = sem("tail_rows_ready")
        s_table = sem("table_ready")
        s_adds = sem("earlier_adds_ready")
        s_wT = sem("weights_transposed")
        s_wTa = sem("weights_copied")
        s_wTd = sem("W1_low_parts_ready")
        s_fb1c = sem("fb1_copied")
        s_slot = [sem(f"slot_in{i}") for i in range(4)]
        s_W1cur = [sem(f"W1cur_in{i}") for i in range(4)]
        s_bias = [sem(f"biases_in{i}") for i in range(4)]
        s_eT = sem("tile_rows_transposed")
        s_eTh = sem("xeT_hi_ready")
        s_eTc = sem("xeT_lo_ready")
        s_goes = sem("goes_ready")
        s_l1 = sem("layer1_done")
        s_reluA = sem("relu_even_ready")
        s_reluD = sem("relu_odd_ready")
        s_l2 = sem("layer2_done")
        s_ye = sem("ye_ready")
        s_ysc = [sem(f"results_scattered{i}") for i in range(4)]
        s_warm = sem("function_table_in")
        s_exp = sem("share_exp_ready")
        s_share = sem("share_ready")
        s_yb = sem("biased_result_ready")
        s_stored = sem("x1_stored")

        adj_g = adj.rearrange("b (h t p) m -> (b h) p t m", h=GPB, p=P)
        x_t = x.rearrange("b (t p) d -> p (b t) d", p=P)
        out_t = out[0:TOK, :].rearrange("(t p) d -> p t d", p=P)

        def wait(eng, s, v):
            if not (isinstance(v, int) and v <= 0):
                eng.wait_ge(s, v)

        class Order:

            def __init__(self, eng, s, links):
                self.eng, self.s, self.links, self.base, self.k = eng, s, links, 0, 0

            def step(self, base):
                self.base, self.k = base, 0

            def link(self, ins):
                self.k += 1
                ins.then_inc(self.s, 1)
                self.eng.wait_ge(self.s, self.base + self.k)

            def end(self):
                assert self.k <= self.links, self.k
                if self.k < self.links:
                    self.eng.sem_inc(self.s, self.links - self.k)

        def first_part(eng, step, last):
            def peeled(g):
                step(g, g % 2, g // 2)
            for g in range(4):
                peeled(g)
            with eng.Fori(2, B - 1) as b:
                for par in range(2):
                    step(b * 2 + par, par, b)
            for g in range(NG - 2, last + 1):
                peeled(g)

        def has(g, lag):
            return not isinstance(g, int) or 0 <= g - lag < NG

        LOOPED = (NTILE - 4) // 4

        def second_part(eng, step, lag):
            for t in range(4):
                step(t, t)
            with eng.Fori(1, 1 + LOOPED) as i:
                for k in range(4):
                    step(i * 4 + k, k)
            for t in range(4 + 4 * LOOPED, NTILE + lag):
                step(t, t % 4)

        def live(t, lag):
            return not isinstance(t, int) or 0 <= t - lag < NTILE

        def added(tiles):
            return tiles * 16 * J

        block = ctx.enter_context(nc.Block())

        def fill_tails(eng, experts):
            for e in experts:
                row = eng.value_load(tail[0:1, e:e + 1], min_val=e * R, max_val=e * R + TOK)
                eng.dma_start(slots[bass.ds(row, TILE), :].rearrange("(p j) c -> p j c", j=J),
                              pad_rows[:, :, :]).then_inc(s_tails, 16)

        @block.sync
        def _(sp):
            sp.dma_start(epss[:, :], eps.to_broadcast([P, 1])).then_inc(s_eps, 16)
            sp.dma_start(x_all[:, 0:TPB, :], x_t[:, 0:TPB, :]).then_inc(s_x0, 16)
            sp.dma_start(adj_in[0][:, :, :], adj_g[0]).then_inc(s_adj[0], 16)
            sp.dma_start(small[0:HC, :], rms_w.rearrange("(c p) -> c p", p=P)).then_inc(s_const, 16)
            sp.dma_start(small[HC:HC + E * HC, :], fb1.rearrange("e (c p) -> (e c) p", p=P)).then_inc(s_const, 16)
            sp.dma_start(small[HC + E * HC:NS, :], Wg[:, :]).then_inc(s_const, 16)
            sp.dma_start(W1_raw, W1[:, :]).then_inc(s_const, 16)
            sp.dma_start(b1s[:, :], b1[None, :].to_broadcast([P, H])).then_inc(s_const, 16)
            sp.dma_start(b2s[:, :], b2[None, :].to_broadcast([P, D])).then_inc(s_const, 16)
            sp.dma_start(bgs[:, :], bg[None, :].to_broadcast([P, E])).then_inc(s_const, 16)
            sp.dma_start(W2s[:, 0:2, :], W2[0:H // 2, :].rearrange("(c p) d -> p c d", p=P)).then_inc(s_const, 16)
            sp.dma_start(W2s[:, 2:4, :], W2[H // 2:H, :].rearrange("(c p) d -> p c d", p=P)).then_inc(s_const, 16)
            sp.dma_start(biases[:, :, CB2:CB2 + D], fb2[None, :, :].to_broadcast([P, E, D])).then_inc(s_fb2, 16)
            sp.dma_start(adj_in[1][:, :, :], adj_g[1]).then_inc(s_adj[1], 16)
            sp.dma_start(x_all[:, TPB:2 * TPB, :], x_t[:, TPB:2 * TPB, :]).then_inc(s_xs, 16)
            sp.dma_start(x_all[:, 2 * TPB:NT, :], x_t[:, 2 * TPB:NT, :]).then_inc(s_xr, 16)
            def load_group(b):
                for par in range(2):
                    g = b * 2 + par
                    sp.wait_ge(s_tp, b * (2 * TPB) + (par - 1) * TPB)
                    src = adj_g[g] if isinstance(g, int) else adj_g[bass.ds(g, 1)].rearrange("o p t m -> (o p) t m")
                    sp.dma_start(adj_in[par][:, :, :], src).then_inc(s_adj[par], 16)
                    if has(g, 4):
                        store_x1(g - 4)

            def store_x1(q):
                sp.wait_ge(s_x1, q + 1)
                a, z = q * GT, (q + 1) * GT
                dst, src = ((out_t[:, a:z, :], x_all[:, a:z, :]) if isinstance(q, int) else
                            (out_t[:, bass.ds(a, GT), :], x_all[:, bass.ds(a, GT), :]))
                sp.dma_start(dst, src).then_inc(s_stored, 16)
            sp.wait_ge(s_made, 1)
            for n in range(SPARE):
                r = E * R + n * TILE
                sp.dma_start(slots[r:r + TILE, :].rearrange("(p j) c -> p j c", j=J),
                             pad_rows2 if n % 2 else pad_rows[:, :, :]).then_inc(s_spare, 16)
            for n in range(2):
                r = TOK + n * TILE
                sp.dma_start(out[r:r + TILE, :].rearrange("(p j) d -> p j d", j=J),
                             pad_rows[:, :, 0:D]).then_inc(s_spare, 16)
            load_group(1)
            with sp.Fori(2, B) as b:
                load_group(b)
            sp.wait_ge(s_tp, TPB * (NG - 1))
            sp.dma_start(F1raw, F1.rearrange("e (c p) d -> p (e c) d", p=P)).then_inc(s_F1, 16)
            sp.wait_ge(s_tp, TPB * NG)
            sp.dma_start(F2raw, F2.rearrange("e d h -> d e h")).then_inc(s_F2, 16)
            for q in range(NG - 4, NG):
                store_x1(q)

            sp.wait_ge(s_tail, 1)
            fill_tails(sp, range(E))
            sp.wait_ge(s_table, 1)
            sp.wait_ge(s_wTa, 2 * E)
            sp.wait_ge(s_wTd, E)
            sp.wait_ge(s_fb1c, 1)
            sp.wait_ge(s_fb2, 16)

            def load_rows(t, k):
                first = sp.value_load(table[0:1, 1, bass.ds(t, 1)], min_val=0,
                                      max_val=E * R + (SPARE - 1) * TILE)
                wait(sp, s_eT, t - 3)
                wait(sp, s_goes, t - 3)
                wait(sp, s_share, t - 3)
                sp.dma_start(slot[k][:, :, :], slots[bass.ds(first, TILE), :]
                             .rearrange("(p j) c -> p j c", j=J)).then_inc(s_slot[k], 16)

            def load_weights(t, k):
                expert = sp.value_load(table[0:1, 0, bass.ds(t, 1)], min_val=0, max_val=E - 1)
                wait(sp, s_l1, 4 * (t - 3))
                sp.dma_start(W1cur[k][:, :, :].bitcast(FP32),
                             W1e[:, bass.ds(expert, 1), :, :].rearrange("p o s w -> p (o s) w").bitcast(FP32)
                             ).then_inc(s_W1cur[k], 16)
                wait(sp, s_reluA, 2 * (t - 3))
                wait(sp, s_reluD, 2 * (t - 3))
                wait(sp, s_yb, t - 3)
                sp.dma_start(bcur[k],
                             biases[:, bass.ds(expert, 1), :].rearrange("p o w -> p (o w)")
                             ).then_inc(s_bias[k], 16)

            load_weights(0, 0)
            sp.wait_ge(s_tails, 16 * E)
            sp.wait_ge(s_spare, 16 * (SPARE + 2))
            sp.wait_ge(s_scat[0], 16 * GT * NG)
            sp.wait_ge(s_scat[1], 16 * GT * NG)
            load_rows(0, 0)

            def load(t, k):
                if not (isinstance(t, int) and t == 0):
                    load_rows(t, k)
                    load_weights(t, k)
            second_part(sp, load, 0)


        @block.tensor
        def _(pe):
            pe.wait_ge(s_ident, 1)

            def expert_weights(e):
                if e == 0:
                    pe.wait_ge(s_F1, 16)
                    pe.wait_ge(s_F2, 16)
                    pe.wait_ge(s_lo, TPB * NG)
                wait(pe, s_wTd, e)
                for c in range(HC):
                    ins = pe.transpose(ps_t[0][:, c * P:(c + 1) * P], F1raw[:, e * HC + c, :], ident[:, :])
                ins.then_inc(s_wT, 1)
                wait(pe, s_wTa, 2 * e)
                for c in range(HC):
                    ins = pe.transpose(ps_t[1][:, c * P:(c + 1) * P], F2raw[:, e, c * P:(c + 1) * P], ident[:, :])
                ins.then_inc(s_wT, 1)

            def three_passes(out_, w_hi, w_lo, m_hi, m_lo, start, stop):
                pe.matmul(out_, w_hi, m_hi, start=start, stop=False)
                pe.matmul(out_, w_hi, m_lo, start=False, stop=False)
                return pe.matmul(out_, w_lo, m_hi, start=False, stop=stop)

            def transpose_rows(buf, m):
                for j in range(GT):
                    ins = pe.transpose(ps_t[m % 2][:, j * P:(j + 1) * P],
                                       adj_in[buf][:, j, m * P:(m + 1) * P], ident[:, :])
                ins.then_inc(s_tp, 1)

            pe.wait_ge(s_epsadd, 4)
            transpose_rows(0, 0)
            transpose_rows(0, 1)

            def step(g, par, b):
                def M(m):
                    if has(g, 0):
                        if par == 0 and m % (TPB // 2) == 0:
                            pe.wait_ge(s_xl, b * 2 + m // (TPB // 2) + 1)
                        pe.wait_ge(s_lo, TPB * g + m + 1)
                        ins = three_passes(ps_agg[par][:, :], xn_hi[:, m, :], xn_lo[:, m, :],
                                           adjT_hi[m % 2][:, :], adjT_lo[m % 2][:, :],
                                           start=(m == 0), stop=(m == TPB - 1))
                        ins.then_inc(s_mm, 1)
                        if m + 2 < TPB:
                            transpose_rows(par, m + 2)
                        elif has(g, -1):
                            if m + 2 == TPB:
                                pe.wait_ge(s_epsadd, 4 * g + 8)
                            transpose_rows(1 - par, m + 2 - TPB)
                    elif isinstance(g, int) and g == NG and m in (0, 2, 4):
                        expert_weights(m // 2)

                def first_layer(tiles):
                    q = g - 1
                    for j in tiles:
                        if j < 2:
                            wait(pe, s_silu, 4 * q - 1 + j)
                        else:
                            pe.wait_ge(s_hb, 4 * q + j - 1)
                        js = slice(j * P, (j + 1) * P)
                        three_passes(ps_h[j % 2][:, :], aggT_hi[:, js], aggT_lo[:, js], W1_hi[:, :], W1_lo[:, :],
                                     start=True, stop=True).then_inc(s_h, 1)

                def transpose_hidden(chunks):
                    q = g - 1
                    for c in chunks:
                        if c >= 2:
                            pe.wait_ge(s_silu, 4 * q + c - 1)
                        for j in range(GT):
                            ins = pe.transpose(ps_h[c % 2][:, j * P:(j + 1) * P],
                                               hn[:, j, c * P:(c + 1) * P], ident[:, :])
                        ins.then_inc(s_hT, 1)

                if has(g, 1):
                    pe.wait_ge(s_agg, g)
                    if isinstance(g, int) and g == 1:
                        pe.wait_ge(s_W1l, 1)
                    first_layer((0, 1))
                M(0)
                if has(g, 1):
                    first_layer((2, 3))
                M(1)
                M(2)
                M(3)
                if isinstance(g, int) and g == NG + 1:
                    expert_weights(3)
                if has(g, 2):
                    q = g - 2
                    pe.wait_ge(s_row1, q + 1)
                    for j in range(GT):
                        ins = pe.transpose(ps_y[:, j * P:(j + 1) * P], rows[par][:, 0, j, 0:D], ident[:, :])
                    ins.then_inc(s_xT, 1)
                M(4)
                if has(g, 2):
                    q = g - 2
                    pe.wait_ge(s_xTc, q + 1)
                    if isinstance(q, int) and q == 0:
                        pe.wait_ge(s_smallc, 1)
                    wait(pe, s_base, q)
                    for j in range(GT):
                        ins = pe.matmul(ps_g[:, j * E:(j + 1) * E], xn2T[:, j * P:(j + 1) * P], WgT,
                                        start=True, stop=True)
                    ins.then_inc(s_gate, 1)
                if isinstance(g, int) and g == NG + 1:
                    expert_weights(4)
                M(5)
                if has(g, 1):
                    pe.wait_ge(s_hn, g)
                    pe.wait_ge(s_hna, g)
                    transpose_hidden((0, 1))
                M(6)
                if has(g, 1):
                    transpose_hidden((2, 3))
                M(7)
                if has(g, 2):
                    q = g - 2
                    pe.wait_ge(s_both, q + 1)
                    pe.matmul(ps_g[:, 0:(GT + 1) * E], earlier[:, :],
                              both[:, :, :].rearrange("p t e -> p (t e)"), start=True, stop=False)
                    for j in range(GT):
                        n = GT - j
                        ins = pe.matmul(ps_g[:, (j + 1) * E:(GT + 1) * E].rearrange("p (n e) -> p n e", e=E),
                                        ones[:, :], both[:, j:j + 1, :].broadcast_to([P, n, E]),
                                        start=False, stop=(j == GT - 1))
                    ins.then_inc(s_rank, 1)
                if isinstance(g, int) and g == NG + 1:
                    for e in range(5, E):
                        expert_weights(e)
                if has(g, 1):
                    q = g - 1
                    pe.wait_ge(s_silu, 4 * q + 4)
                    wait(pe, s_x1, q)
                    for j in range(GT):
                        for c in range(HC):
                            ins = pe.matmul(ps_y[:, j * P:(j + 1) * P], siluT[:, c, j * P:(j + 1) * P],
                                            W2s[:, c, :], start=(c == 0), stop=(c == HC - 1))
                    ins.then_inc(s_y, 1)
                if isinstance(g, int) and g == 0:
                    pe.wait_ge(s_const, 16 * 9)
                    pe.transpose(ps_g[:, 0:NS], small[:, :], ident[0:NS, 0:NS]).then_inc(s_smallT, 1)
            first_part(pe, step, NG + 1)

            ps_e = [ps_t[0], ps_t[1]]
            ps_1 = [ps_agg[0], ps_h[0], ps_h[1], ps_agg[1]]
            ps_2 = [ps_y, ps_g]

            def expert_of(t):
                return pe.value_load(table[0:1, 0, bass.ds(t, 1)], min_val=0, max_val=E - 1)

            def of(w, expert):
                return w[:, bass.ds(expert, 1), :].rearrange("p o w -> p (o w)")

            pe.wait_ge(s_table, 1)
            pe.wait_ge(s_wTa, 2 * E)
            pe.wait_ge(s_wTd, E)

            def tile(t, k):
                if live(t, 0):
                    pe.wait_ge(s_slot[k], 16 * (t // 4 + 1) if isinstance(t, int) else t * 4 + (16 - 4 * k))
                    wait(pe, s_eTc, t - 1)
                    for j in range(J):
                        ins = pe.transpose(ps_e[k % 2][:, j * P:(j + 1) * P], slot[k][:, j, 0:D], ident[:, :])
                    ins.then_inc(s_eT, 1)
                if live(t, 1):
                    u, ku = t - 1, (k - 1) % 4
                    pe.wait_ge(s_eTc, u + 1)
                    pe.wait_ge(s_bias[ku],
                               16 * (u // 4 + 1) if isinstance(u, int) else u * 4 + (16 - 4 * ku))
                    pe.wait_ge(s_W1cur[ku],
                               16 * (u // 4 + 1) if isinstance(u, int) else u * 4 + (16 - 4 * ku))
                    for c in range(HC):
                        wait(pe, s_reluD if c % 2 else s_reluA, 2 * (u - 1) + c // 2 + 1)
                        cs = slice(c * P, (c + 1) * P)
                        three_passes(ps_1[c][:, 0:TILE], W1cur[ku][:, 0, cs], W1cur[ku][:, 1, cs],
                                     xeT_hi[ku % 2], xeT_lo[ku % 2], start=True, stop=True).then_inc(s_l1, 1)
                if live(t, 2):
                    u, ku = t - 2, (k - 2) % 4
                    pe.wait_ge(s_reluA, 2 * u + 2)
                    pe.wait_ge(s_reluD, 2 * u + 2)
                    wait(pe, s_yb, u - 1)
                    expert = expert_of(u)
                    for j in range(J):
                        for c in range(HC):
                            ins = pe.matmul(ps_2[ku % 2][:, j * P:(j + 1) * P], hT[ku % 2][:, c, j * P:(j + 1) * P],
                                            of(W2e, expert)[:, c * D:(c + 1) * D],
                                            start=(c == 0), stop=(c == HC - 1))
                    ins.then_inc(s_l2, 1)
            second_part(pe, tile, 2)

        @block.scalar
        def _(act):
            act.wait_ge(s_made, 1)
            act.activation(share_e[0][:, 0:1], zeros[:, 0:1], ACT.Silu).then_inc(s_warm, 1)

            def copy_weights(e):
                for i, dst in enumerate((W1e[:, e, 0, :], W2e[:, e, :])):
                    act.wait_ge(s_wT, 2 * e + i + 1)
                    act.activation(dst, ps_t[i][:, :], ACT.Copy).then_inc(s_wTa, 1)

            def normalise(b, half):
                if half == 0:
                    act.wait_ge(s_rs1, b + 1)
                    wait(act, s_xl, b * 2)
                for j in range(half * GT, (half + 1) * GT):
                    t = b * TPB + j
                    src = x_all[:, t, :] if isinstance(t, int) else x_all[:, bass.ds(t, 1), :].rearrange("p o d -> p (o d)")
                    ins = act.activation(xn[:, j, :], src, ACT.Identity, bias=shift1[:, j:j + 1], scale=rstd1[:, j:j + 1])
                ins.then_inc(s_xn, 1)

            def high_half(b, i):
                act.wait_ge(s_xn, b * 2 + i + 1)
                h = slice(i * (TPB // 2), (i + 1) * (TPB // 2))
                act.activation(xn_hi[:, h, :], xn[:, h, :], ACT.Copy).then_inc(s_xh, 1)

            def high_part(n, m):
                act.wait_ge(s_tp, n + 1)
                act.activation(adjT_hi[m % 2][:, :], ps_t[m % 2][:, :], ACT.Copy).then_inc(s_hi, 1)

            for i in range(2):
                normalise(0, i)
                high_half(0, i)
            high_part(0, 0)
            high_part(1, 1)

            def step(g, par, b):
                def evac(m):
                    if has(g, 0 if m < TPB else -1):
                        high_part(TPB * g + m, m)
                    elif isinstance(g, int) and g == NG and m in (2, 4, 6):
                        copy_weights(m // 2 - 1)

                def square(j):
                    if has(g, 1):
                        if isinstance(g, int) and g == 1 and j == 0:
                            act.wait_ge(s_spare, 16 * (SPARE + 2))
                        if j == 0:
                            wait(act, s_rms, g - 1)
                            wait(act, s_hT, 4 * (g - 1))
                        act.wait_ge(s_hb, 4 * (g - 1) + j + 1)
                        act.activation(hn[:, j, :], hb[:, j, :], ACT.Square,
                                       accum_out=ss[:, j:j + 1]).then_inc(s_ss, 1)

                def silu(c):
                    if has(g, 1):
                        if c == 0:
                            wait(act, s_y, g - 1)
                        act.wait_ge(s_hT, 4 * (g - 1) + c + 1)
                        act.activation(siluT[:, c, :], ps_h[c % 2][:, :], ACT.Silu,
                                       scale=rmsT[:, c:c + 1]).then_inc(s_silu, 1)

                square(0)
                evac(2)
                square(1)
                evac(3)
                square(2)
                square(3)
                evac(4)
                evac(5)
                if isinstance(g, int) and g == NG + 1:
                    copy_weights(3)
                if has(g, 2):
                    q = g - 2
                    act.wait_ge(s_xT, q + 1)
                    wait(act, s_gate, q)
                    act.activation(xn2T[:, :], ps_y[:, :], ACT.Copy).then_inc(s_xTc, 1)
                if isinstance(g, int) and g == 0:
                    act.wait_ge(s_const, 16 * 9)
                    act.activation(W1_hi[:, :], W1_raw, ACT.Copy).then_inc(s_W1h, 1)
                if isinstance(g, int) and g == 1:
                    act.wait_ge(s_smallc, 1)
                    act.activation(biases[:, :, CB1:CB1 + HC], fb1T.rearrange("p (e c) -> p e c", c=HC),
                                   ACT.Copy).then_inc(s_fb1c, 1)
                if has(g, 1):
                    act.wait_ge(s_rms, g)
                    for j in range(GT // 2, GT):
                        ins = act.activation(hn[:, j, :], hb[:, j, :], ACT.Copy, scale=rms_rstd[:, j:j + 1])
                    ins.then_inc(s_hna, 1)
                evac(6)
                if par == 1 and has(g, -1):
                    normalise(b + 1, 0)
                evac(7)
                silu(0)
                silu(1)
                evac(8)
                silu(2)
                silu(3)
                if par == 1 and has(g, -1):
                    high_half(b + 1, 0)
                evac(9)
                if has(g, 0):
                    act.wait_ge(s_mm, TPB * g + TPB)
                    act.activation(aggT_hi[:, :], ps_agg[par][:, :], ACT.Copy).then_inc(s_aggh, 1)
                if par == 1 and has(g, -1):
                    normalise(b + 1, 1)
                    high_half(b + 1, 1)
                if has(g, 2):
                    q = g - 2
                    act.wait_ge(s_row1, q + 1)
                    act.activation(rows[par][:, 1, :, 0:D], rows[par][:, 0, :, 0:D], ACT.Copy).then_inc(s_row2, 1)
                if isinstance(g, int) and g == NG + 1:
                    for e in range(4, E):
                        copy_weights(e)
            first_part(act, step, NG + 1)

            act.activation(share_e[0][:, 0:1], zeros[:, 0:1], ACT.Exp).then_inc(s_warm, 1)
            act.wait_ge(s_warm, 2)

            ps_1 = [ps_agg[0], ps_h[0], ps_h[1], ps_agg[1]]

            ps_e = [ps_t[0], ps_t[1]]

            def tile(t, k):
                if live(t, 0):
                    act.wait_ge(s_eT, t + 1)
                    wait(act, s_l1, 4 * (t - 1))
                    act.activation(xeT_hi[k % 2], ps_e[k % 2][:, 0:TILE], ACT.Copy).then_inc(s_eTh, 1)
                    act.wait_ge(s_slot[k], 16 * (t // 4 + 1) if isinstance(t, int) else t * 4 + (16 - 4 * k))
                    wait(act, s_share, t - 3)
                    act.activation(share_e[k][:, :], slot[k][:, :, GAP], ACT.Exp).then_inc(s_exp, 1)
                if live(t, 1):
                    u, ku = t - 1, (k - 1) % 4
                    for c in (0, 2):
                        act.wait_ge(s_l1, 4 * u + c + 1)
                        wait(act, s_l2, u - 1)
                        act.activation(hT[ku % 2][:, c, :], ps_1[c][:, 0:TILE], ACT.Relu,
                                       bias=bcur[ku][:, CB1 + c:CB1 + c + 1]).then_inc(s_reluA, 1)
                if live(t, 2):
                    u, ku = t - 2, (k - 2) % 4
                    act.wait_ge(s_share, u + 1)
                    act.wait_ge(s_yb, u + 1)
                    wait(act, s_ysc[ku], added(u // 4) if isinstance(u, int) else (u - ku) * (4 * J))
                    for j in range(J):
                        ins = act.activation(ye[ku][:, j, :], yb[ku % 2][:, j, :], ACT.Copy, scale=share[ku][:, j:j + 1])
                    ins.then_inc(s_ye, 1)
            second_part(act, tile, 2)

        @block.gpsimd
        def _(pool):
            order = Order(pool, s_pool, 6)
            order.step(0)
            pool.memset(ident[:, :], 0.0)
            pool.memset(minus_half[:, :], -0.5)
            pool.memset(ln_eps[:, :], 1e-5)
            pool.memset(zeros[:, :], 0.0)
            pool.memset(rms_eps[:, :], 1e-6 * H)
            pool.memset(earlier[:, :], 1.0)
            pool.memset(pad_rows[:, :, :], 0.0)
            pool.memset(pad_rows2, 0.0)
            order.link(pool.memset(ones[:, :], 1.0))
            pool.affine_select(out=ident[:, :], in_=ident[:, :], compare_op=ALU.not_equal, fill=1.0, base=0,
                               pattern=[[-1, P]], channel_multiplier=1).then_inc(s_ident, 1)
            pool.affine_select(out=earlier[:, :], in_=earlier[:, :], compare_op=ALU.is_gt, fill=0.0, base=0,
                               pattern=[[1, P]], channel_multiplier=-1)
            pool.iota(token_id[:, :], [[P, NT]], base=0, channel_multiplier=1,
                      allow_small_or_imprecise_dtypes=True)
            for i in range(2):
                for c in range(2):
                    pool.memset(rows[i][:, c, :, CHOICE:CHOICE + 1], float(c))
            pool.iota(falling[:, :, :], [[0, GT], [-1, E]], base=E, channel_multiplier=0,
                      allow_small_or_imprecise_dtypes=True)
            pool.iota(base0[:, :], [[R, E]], base=0, channel_multiplier=0, allow_small_or_imprecise_dtypes=True)
            pool.iota(step_k[:, :, :], [[0, E], [TILE, MAXT]], base=0, channel_multiplier=0,
                      allow_small_or_imprecise_dtypes=True)
            pool.iota(t_idx[:, :, :], [[1, NTILE], [0, E]], base=0, channel_multiplier=0,
                      allow_small_or_imprecise_dtypes=True)
            pool.iota(before[:, :, :], [[16 * J, -(-NTILE // 4)], [0, 4]], base=0, channel_multiplier=0,
                      allow_small_or_imprecise_dtypes=True)
            pool.iota(upto[:, :, :], [[1, E], [-1, E]], base=0, channel_multiplier=0,
                      allow_small_or_imprecise_dtypes=True)
            pool.iota(pad_rows2[:, :, ID], [[1, J]], base=TOK + TILE, channel_multiplier=J,
                      allow_small_or_imprecise_dtypes=True)
            order.link(pool.iota(pad_rows[:, :, ID], [[1, J]], base=TOK, channel_multiplier=J,
                                 allow_small_or_imprecise_dtypes=True))
            pool.memset(both_pad := both[:, GT:GT + 1, :], 0.0).then_inc(s_made, 1)
            pool.wait_ge(s_eps, 16)
            order.link(pool.tensor_scalar(eps_ident[:, :], ident[:, :], epss[:, 0:1], 1.0, ALU.mult, ALU.mult))
            def inv_sqrt(square_, eps_, scratch, result, n, s_done):
                order.link(pool.tensor_tensor(scratch, square_, eps_[:, 0:n], ALU.add))
                pool.tensor_tensor(result, scratch, minus_half[:, 0:n], ALU.pow).then_inc(s_done, 1)

            def ln1_factors():
                order.link(pool.tensor_tensor(ve1[:, :], mv1[:, :, 1], ln_eps[:, :], ALU.add))
                order.link(pool.tensor_tensor(rstd1[:, :], ve1[:, :], minus_half[:, :], ALU.pow))
                order.link(pool.tensor_tensor(ve1[:, :], mv1[:, :, 0], rstd1[:, :], ALU.mult))
                pool.tensor_tensor(shift1[:, :], zeros[:, :], ve1[:, :], ALU.subtract).then_inc(s_rs1, 1)

            def add_eps(g, par, b):
                pool.wait_ge(s_adj[par], 16 * b + 16)
                for j in range(GT):
                    col = (par * GT + j) * P
                    pool.tensor_tensor(adj_in[par][:, j, col:col + P], adj_in[par][:, j, col:col + P],
                                       eps_ident[:, :], ALU.add).then_inc(s_epsadd, 1)

            def x_plus_b2(b):
                xv = x_all[:, bass.ds(b * TPB, TPB), :] if not isinstance(b, int) else x_all[:, b * TPB:(b + 1) * TPB, :]
                pool.tensor_tensor(xv, xv, b2s[:, None, :].broadcast_to([P, TPB, D]), ALU.add).then_inc(s_xb, 1)

            pool.wait_ge(s_mv1, 1)
            ln1_factors()
            add_eps(0, 0, 0)
            order.end()
            def scatter_rows(g, par, c):
                for j in range(GT):
                    pool.indirect_dma_start(
                        out=slots, out_offset=bass.IndirectOffsetOnAxis(ap=dest[1 - par][:, c, j:j + 1], axis=0),
                        in_=rows[1 - par][:, c, j, :], in_offset=None,
                        bounds_check=E * R - 1, oob_is_err=True).then_inc(s_scat[1 - par], 16)

            def step(g, par, b):
                order.step((g + 1) * 6)
                if has(g, 3):
                    pool.wait_ge(s_dest, g - 2)
                    pool.wait_ge(s_row2, g - 2)
                if has(g, 2):
                    q = g - 2
                    pool.wait_ge(s_mv2, q + 1)
                    wait(pool, s_row1, q)
                    inv_sqrt(mv2[:, :, 1], ln_eps, ve2[:, :], rstd2[:, :], GT, s_rs2)
                if has(g, 1):
                    q = g - 1
                    pool.wait_ge(s_ss, 4 * q + 4)
                    wait(pool, s_hn, q)
                    wait(pool, s_hna, q)
                    inv_sqrt(ss[:, :], rms_eps, rms_var[:, :], rms_rstd[:, :], GT, s_rms)
                if has(g, -1):
                    add_eps(g + 1, 1 - par, b + par)
                if isinstance(g, int) and g == 0:
                    pool.wait_ge(s_const, 16 * 9)
                if par == 0 and has(g, 0):
                    pool.wait_ge(s_xn, b * 2 + 2)
                    pool.sem_inc(s_turn, 1)
                    x_plus_b2(b)
                if has(g, 3):
                    for c in range(2):
                        if not (isinstance(g, int) and g == NG + 1 and c == 0):
                            scatter_rows(g, par, c)
                if isinstance(g, int) and g == NG:
                    pool.wait_ge(s_dest, g - 1)
                    pool.wait_ge(s_row2, g - 1)
                    scatter_rows(g + 1, 1 - par, 0)
                if par == 0 and has(g, -2):
                    pool.wait_ge(s_mv1, b + 2)
                    ln1_factors()
                order.end()
            first_part(pool, step, NG + 2)

            pool.wait_ge(s_stored, 16 * NG)
            pool.wait_ge(s_spare, 16 * (SPARE + 2))
            pool.wait_ge(s_adds, 1)

            def add_results(t, k):
                if live(t, 2):
                    u, ku = t - 2, (k - 2) % 4
                    pool.wait_ge(s_ye, u + 1)
                    pool.wait_ge(s_goes, u + 1)
                    first_two = isinstance(u, int) and u < 2
                    if not (isinstance(u, int) and u == 0):
                        need = pool.value_load(earlier_adds[0:1, bass.ds(u - 1, 1)], min_val=16 * J,
                                               max_val=added(NTILE // 4 + 1))
                        pool.wait_ge(s_ysc[(ku - 1) % 4], need)
                    if not first_two:
                        prev = u - 2
                        pool.wait_ge(s_ysc[(ku - 2) % 4],
                                     added(prev // 4 + 1) if isinstance(u, int)
                                     else prev * (4 * J) + (4 - (ku - 2) % 4) * (4 * J))
                    pool.sem_inc(s_turn, 1)
                    for j in range(J):
                        pool.indirect_dma_start(
                            out=out, out_offset=bass.IndirectOffsetOnAxis(ap=goes[ku][:, j:j + 1], axis=0),
                            in_=ye[ku][:, j, :], in_offset=None, bounds_check=TOK + 2 * TILE - 1,
                            compute_op=ALU.add).then_inc(s_ysc[ku], 16)
            second_part(pool, add_results, 2)
            for k in range(4):
                pool.wait_ge(s_ysc[k], added((NTILE + 3 - k) // 4))

        @block.vector
        def _(dve):
            order = Order(dve, s_dve, 22)
            order.step(0)

            def token_tile(t):
                return x_all[:, t, :] if isinstance(t, int) else x_all[:, bass.ds(t, 1), :].rearrange("p o d -> p (o d)")

            def ln1_stats(b, half):
                for j in range(half * GT, (half + 1) * GT):
                    ins = dve.bn_stats(st1[:, j, :], token_tile(b * TPB + j))
                order.link(ins)

            def ln1_aggregate(b):
                for j in range(TPB):
                    ins = dve.bn_aggr(mv1[:, j, :], st1[:, j, :])
                ins.then_inc(s_mv1, 1)

            dve.wait_ge(s_x0, 16)
            ln1_stats(0, 0)
            ln1_stats(0, 1)
            ln1_aggregate(0)
            dve.wait_ge(s_made, 1)
            dve.tensor_copy(base[:, :], base0[:, :])
            dve.tensor_scalar(upto[:, :, :], upto[:, :, :], 0.0, None, ALU.is_ge)

            def low_half(b, i):
                dve.wait_ge(s_xh, b * 2 + i + 1)
                h = slice(i * (TPB // 2), (i + 1) * (TPB // 2))
                dve.tensor_tensor(xn_lo[:, h, :], xn[:, h, :], xn_hi[:, h, :].bitcast(FP32),
                                  ALU.subtract).then_inc(s_xl, 1)

            def low_part(n, m):
                dve.wait_ge(s_hi, n + 1)
                dve.tensor_tensor(adjT_lo[m % 2][:, :], ps_t[m % 2][:, :], adjT_hi[m % 2][:, :].bitcast(FP32),
                                  ALU.subtract).then_inc(s_lo, 1)

            def low_weights(e):
                dve.wait_ge(s_wTa, 2 * e + 1)
                dve.tensor_tensor(W1e[:, e, 1, :], ps_t[0][:, :], W1e[:, e, 0, :].bitcast(FP32),
                                  ALU.subtract).then_inc(s_wTd, 1)

            low_half(0, 0)
            low_half(0, 1)
            low_part(0, 0)
            low_part(1, 1)
            order.end()

            def step(g, par, b):
                order.step((g + 1) * 22)

                def evac(m):
                    if has(g, 0 if m < TPB else -1):
                        low_part(TPB * g + m, m)
                    elif isinstance(g, int) and g == NG and m in (2, 4, 6):
                        low_weights(m // 2 - 1)

                def add_b1(tiles):
                    if has(g, 1):
                        for j in tiles:
                            dve.wait_ge(s_h, 4 * (g - 1) + j + 1)
                            dve.tensor_tensor(hb[:, j, :], ps_h[j % 2][:, :], b1s[:, :], ALU.add).then_inc(s_hb, 1)

                def best(c, src):
                    order.link(dve.reduce_max(top[:, c, :], src[:, :, :], AX.X))
                    order.link(dve.tensor_tensor(tied[:, :, :], src[:, :, :],
                                                 top[:, c, :, None].broadcast_to([P, GT, E]), ALU.is_equal))
                    order.link(dve.tensor_tensor(tied[:, :, :], tied[:, :, :], falling[:, :, :], ALU.mult))
                    order.link(dve.reduce_max(first_of[:, c, :], tied[:, :, :], AX.X))
                    order.link(dve.tensor_tensor(onehot[:, c, :, :], falling[:, :, :],
                                                 first_of[:, c, :, None].broadcast_to([P, GT, E]), ALU.is_equal))

                add_b1((0, 1))
                if has(g, 2):
                    q = g - 2
                    dve.wait_ge(s_x1, q + 1)
                    dve.sem_inc(s_turn_dve, 1)
                    for j in range(GT):
                        ins = dve.bn_stats(st2[:, j, :], token_tile(q * GT + j))
                    order.link(ins)
                    dve.sem_inc(s_turn_dve, 1)
                evac(2)
                if has(g, 2):
                    for j in range(GT):
                        ins = dve.bn_aggr(mv2[:, j, :], st2[:, j, :])
                    ins.then_inc(s_mv2, 1)
                if isinstance(g, int) and g == NG + 1:
                    low_weights(3)
                add_b1((2, 3))
                evac(3)
                if has(g, 2):
                    q = g - 2
                    wait(dve, s_scat[par], (q // 2) * 128 if isinstance(q, int) else (q - par) * 64)
                    ids = token_id[:, q * GT:(q + 1) * GT] if isinstance(q, int) else token_id[:, bass.ds(q * GT, GT)]
                    dve.tensor_copy(rows[par][:, :, :, ID], ids[:, None, :].broadcast_to([P, 2, GT]))
                    dve.wait_ge(s_rs2, q + 1)
                    for j in range(GT):
                        ins = dve.tensor_scalar(rows[par][:, 0, j, 0:D], token_tile(q * GT + j), mv2[:, j, 0:1],
                                                rstd2[:, j:j + 1], ALU.subtract, ALU.mult)
                    ins.then_inc(s_row1, 1)
                evac(4)
                if isinstance(g, int) and g == 0:
                    dve.wait_ge(s_W1h, 1)
                    dve.tensor_tensor(W1_lo[:, :], W1_raw, W1_hi[:, :].bitcast(FP32), ALU.subtract).then_inc(s_W1l, 1)
                evac(5)
                if par == 0 and has(g, -2):
                    if isinstance(b, int) and b <= 1:
                        dve.wait_ge(s_xs if b == 0 else s_xr, 16)
                    ln1_stats(b + 1, 0)
                if has(g, 1):
                    q = g - 1
                    dve.wait_ge(s_rms, q + 1)
                    wait(dve, s_hT, 4 * q)
                    for j in range(GT // 2):
                        ins = dve.tensor_scalar(hn[:, j, :], hb[:, j, :], rms_rstd[:, j:j + 1], None, ALU.mult)
                    ins.then_inc(s_hn, 1)
                evac(6)
                if has(g, 2):
                    q = g - 2
                    dve.wait_ge(s_gate, q + 1)
                    order.link(dve.tensor_tensor(score[:, :, :], ps_g[:, 0:GT * E].rearrange("p (t e) -> p t e", e=E),
                                                 bgs[:, None, :].broadcast_to([P, GT, E]), ALU.add))
                    best(0, score)
                evac(7)
                if has(g, 2):
                    order.link(dve.scalar_tensor_tensor(rest[:, :, :], onehot[:, 0, :, :], -BIG, score[:, :, :],
                                                        ALU.mult, ALU.add))
                    best(1, rest)
                    dve.tensor_tensor(both[:, 0:GT, :], onehot[:, 0, :, :], onehot[:, 1, :, :], ALU.add).then_inc(s_both, 1)
                    order.link(dve.tensor_tensor(rows[par][:, :, :, GAP], top[:, 1, None, :].broadcast_to([P, 2, GT]),
                                                 top[:, 0, None, :].broadcast_to([P, 2, GT]), ALU.subtract))
                if isinstance(g, int) and g == NG + 1:
                    low_weights(4)
                evac(8)
                if has(g, 2):
                    q = g - 2
                    dve.wait_ge(s_rank, q + 1)
                    order.link(dve.tensor_tensor(place[:, :, :], ps_g[:, 0:GT * E].rearrange("p (t e) -> p t e", e=E),
                                                 base[:, None, :].broadcast_to([P, GT, E]), ALU.add))
                    dve.tensor_tensor(base[:, :], base[:, :], ps_g[:, GT * E:(GT + 1) * E], ALU.add).then_inc(s_base, 1)
                    order.link(dve.tensor_tensor(picked[:, :, :, :], onehot[:, :, :, :],
                                                 place[:, None, :, :].broadcast_to([P, 2, GT, E]), ALU.mult))
                    wait(dve, s_scat[par], (q // 2) * 128 if isinstance(q, int) else (q - par) * 64)
                    with nc.allow_low_precision(reason="sums of whole numbers below 2**24, one of them not zero"):
                        dve.tensor_reduce(dest[par][:, :, :].rearrange("p c t -> p (c t)"),
                                          picked[:, :, :, :].rearrange("p c t e -> p (c t) e"),
                                          AX.X, ALU.add).then_inc(s_dest, 1)
                if par == 0 and has(g, -2):
                    ln1_stats(b + 1, 1)
                    dve.wait_ge(s_rs1, b + 1)
                    dve.sem_inc(s_turn_dve, 1)
                if par == 1 and has(g, -1):
                    low_half(b + 1, 0)
                evac(9)
                if has(g, 0):
                    dve.wait_ge(s_aggh, g + 1)
                    dve.tensor_tensor(aggT_lo[:, :], ps_agg[par][:, :], aggT_hi[:, :].bitcast(FP32),
                                      ALU.subtract).then_inc(s_agg, 1)
                if par == 0 and has(g, -2):
                    ln1_aggregate(b + 1)
                if par == 1 and has(g, -1):
                    low_half(b + 1, 1)
                if has(g, 1):
                    q = g - 1
                    dve.wait_ge(s_y, q + 1)
                    dve.wait_ge(s_xb, b + par)
                    xv = x_all[:, q * GT:(q + 1) * GT, :] if isinstance(q, int) else x_all[:, bass.ds(q * GT, GT), :]
                    dve.tensor_tensor(xv, ps_y[:, :].rearrange("p (t d) -> p t d", d=D), xv, ALU.add).then_inc(s_x1, 1)
                if isinstance(g, int) and g == 0:
                    dve.wait_ge(s_smallT, 1)
                    dve.tensor_scalar(rmsT, ps_g[:, 0:HC], float(H) ** 0.5, None, ALU.mult)
                    dve.tensor_copy(smallT[:, HC:NS], ps_g[:, HC:NS]).then_inc(s_smallc, 1)
                order.end()
            first_part(dve, step, NG + 1)

            order.step((NG + 3) * 22)
            dve.wait_ge(s_base, NG)
            dve.tensor_copy(tail[:, :], base[0:1, :]).then_inc(s_tail, 1)
            order.link(dve.tensor_tensor(t_cnt[:, :], base[0:1, :], base0[0:1, :], ALU.subtract))
            order.link(dve.tensor_tensor(t_gt[:, :, :], t_cnt[:, :, None].broadcast_to([1, E, MAXT]), step_k[:, :, :], ALU.is_gt))
            order.link(dve.tensor_reduce(t_nt[:, :], t_gt[:, :, :], AX.X, ALU.add))
            low_weights(5)
            order.link(dve.tensor_tensor(t_m[:, :, :], t_nt[:, None, :].broadcast_to([1, E, E]), upto[:, :, :], ALU.mult))
            order.link(dve.tensor_reduce(t_end[:, :], t_m[:, :, :], AX.X, ALU.add))
            low_weights(6)
            order.link(dve.tensor_tensor(t_ge[:, :, :], t_idx[:, :, :], t_end[:, None, :].broadcast_to([1, NTILE, E]), ALU.is_ge))
            order.link(dve.tensor_tensor(t_gn[:, :, :], t_ge[:, :, :], t_nt[:, None, :].broadcast_to([1, NTILE, E]), ALU.mult))
            dve.tensor_reduce(t_e[:, :], t_ge[:, :, :], AX.X, ALU.add)
            order.link(dve.tensor_reduce(t_s[:, :], t_gn[:, :, :], AX.X, ALU.add))
            order.link(dve.tensor_tensor(t_o[:, :], t_idx[:, :, 0], t_s[:, :], ALU.subtract))
            order.link(dve.tensor_scalar(t_o[:, :], t_o[:, :], float(TILE), None, ALU.mult))
            dve.scalar_tensor_tensor(table[:, 1, :], t_e[:, :], float(R), t_o[:, :], ALU.mult, ALU.add)
            dve.tensor_scalar(table[:, 0, :], t_e[:, :], float(E - 1), None, ALU.min).then_inc(s_table, 1)
            low_weights(7)
            order.link(dve.tensor_tensor(t_new[:, :], t_s[:, :], t_idx[:, :, 0], ALU.is_equal))
            ins = dve.scalar_tensor_tensor(t_wait[:, :], t_new[:, 1:NTILE], float(16 * J),
                                     before[:, :, :].rearrange("o a k -> o (a k)")[:, 0:NTILE - 1],
                                     ALU.mult, ALU.add)
            order.link(ins)
            dve.tensor_scalar(earlier_adds[:, :], t_wait[:, :], float(16 * J), None, ALU.max).then_inc(s_adds, 1)
            order.end()

            ps_e = [ps_t[0], ps_t[1]]
            ps_1 = [ps_agg[0], ps_h[0], ps_h[1], ps_agg[1]]
            ps_2 = [ps_y, ps_g]

            shares = Order(dve, s_dve2, 2)

            def tile(t, k):
                if live(t, 0):
                    dve.wait_ge(s_eT, t + 1)
                    wait(dve, s_ysc[k], added(t // 4) if isinstance(t, int) else (t - k) * (4 * J))
                    dve.tensor_copy(goes[k][:, :], slot[k][:, :, ID]).then_inc(s_goes, 1)
                    dve.wait_ge(s_eTh, t + 1)
                    dve.tensor_tensor(xeT_lo[k % 2], ps_e[k % 2][:, 0:TILE],
                                      xeT_hi[k % 2].bitcast(FP32), ALU.subtract).then_inc(s_eTc, 1)
                    shares.step(t * 2)
                    dve.wait_ge(s_exp, t + 1)
                    dve.tensor_scalar(share_d[k][:, :], share_e[k][:, :], 1.0, None, ALU.add)
                    shares.link(dve.scalar_tensor_tensor(share_n[k][:, :], share_e[k][:, :], -1.0, slot[k][:, :, CHOICE],
                                                         ALU.add, ALU.mult))
                    shares.link(dve.reciprocal(share_d[k][:, :], share_d[k][:, :]))
                    wait(dve, s_ye, t - 3)
                    dve.scalar_tensor_tensor(share[k][:, :], share_n[k][:, :], 1.0, share_d[k][:, :],
                                             ALU.add, ALU.mult).then_inc(s_share, 1)
                if live(t, 1):
                    u, ku = t - 1, (k - 1) % 4
                    for c in (1, 3):
                        dve.wait_ge(s_l1, 4 * u + c + 1)
                        wait(dve, s_l2, u - 1)
                        dve.tensor_scalar(hT[ku % 2][:, c, :], ps_1[c][:, 0:TILE],
                                          bcur[ku][:, CB1 + c:CB1 + c + 1], 0.0,
                                          ALU.add, ALU.max).then_inc(s_reluD, 1)
                if live(t, 2):
                    u, ku = t - 2, (k - 2) % 4
                    dve.wait_ge(s_l2, u + 1)
                    wait(dve, s_ye, u - 1)
                    dve.tensor_tensor(yb[ku % 2][:, :, :], ps_2[ku % 2][:, 0:TILE].rearrange("p (j d) -> p j d", d=D),
                                      bcur[ku][:, None, CB2:CB2 + D].broadcast_to([P, J, D]), ALU.add).then_inc(s_yb, 1)
            second_part(dve, tile, 2)



_INS = ["x", "adj", "L0_gnn_epsilon", "L0_gnn_W1", "L0_gnn_b1", "L0_gnn_rms_weight", "L0_gnn_W2", "L0_gnn_b2",
        "L0_ffn_Wg", "L0_ffn_bg", "L0_ffn_W1", "L0_ffn_b1", "L0_ffn_W2", "L0_ffn_b2"]


def kernel(**inputs):
    import concourse.bacc as bacc
    from concourse.bass_utils import run_bass_kernel_spmd

    nc = bacc.Bacc("TRN2", target_bir_lowering=False, num_devices=1)
    arrays, args = {}, []
    for name in _INS:
        a = np.ascontiguousarray(inputs[name])
        if a.ndim == 0:
            a = a.reshape(1, 1)
        arrays[f"in_{name}"] = a
        args.append(nc.dram_tensor(f"in_{name}", a.shape, mybir.dt.from_np(a.dtype), kind="ExternalInput").ap())
    shape = inputs["x"].shape
    tokens = shape[0] * shape[1]
    args.append(nc.dram_tensor("out_0", (tokens + 2 * TILE, shape[2]), FP32, kind="ExternalOutput").ap())
    build(nc, *args)
    r = run_bass_kernel_spmd(nc, [arrays], core_ids=[0])
    return r.results[0]["out_0"][:tokens].reshape(shape)
```
